# Optimizing a Trainium2 kernel written in Bass

```python
import numpy as np
import jax
import jax.numpy as jnp

def _softmax(x, axis=-1):
    return jax.nn.softmax(x, axis=axis)

def _gelu(x):
    return jax.nn.gelu(x, approximate=True)

def _silu(x):
    return jax.nn.silu(x)

def _sigmoid(x):
    return jax.nn.sigmoid(x)

def _layernorm(x, axis=-1, eps=1e-05):
    m = jnp.mean(x, axis=axis, keepdims=True)
    v = jnp.var(x, axis=axis, keepdims=True)
    return (x - m) / jnp.sqrt(v + eps)

def _scatter_add(tgt, idx, src, axis=0):
    return tgt.at[idx].add(src)

def _segment_sum(src, seg, n):
    return jax.ops.segment_sum(src, seg, n)
kernel_name = 'mk_adaln_ffn_d2_seqx_r8_6e1f3c'

def setup_inputs(seed: int=0):
    np.random.seed(seed)
    _w = jnp.asarray

    def _rec_inputs():
        import jax
        import jax.numpy as jnp
        _rk = jax.random.key(seed)
        x = 0.0001044 + 1 * jax.random.normal(jax.random.fold_in(_rk, 1), (4, 256, 128), jnp.float32)
        _lenS = 256 - jax.random.randint(jax.random.fold_in(_rk, 7), (4,), 0, max(1, 256 // 4) + 1, jnp.int32)
        _lenS2 = 256 - jax.random.randint(jax.random.fold_in(_rk, 8), (4,), 0, max(1, 256 // 4) + 1, jnp.int32)
        cond_1024 = 0.00141218 + 0.997886 * jax.random.normal(jax.random.fold_in(_rk, 11), (4, 128), jnp.float32)
        return (x, cond_1024)
    x, cond_1024 = _rec_inputs()

    def _L0_cond_setup():
        import jax, jax.numpy as jnp
        import numpy as np
        B, T, C = (64, 64, 128)
        key = jax.random.key(seed)
        ks = jax.random.split(key, 17)
        s_in = 1.0 / np.sqrt(C)

        def lin(kw, kb, fan_in):
            s = 1.0 / np.sqrt(fan_in)
            W = jax.random.uniform(kw, (C, fan_in), jnp.float32, -s, s)
            b = jax.random.uniform(kb, (C,), jnp.float32, -s, s)
            return (W, b)
        Wxz, bxz = lin(ks[0], ks[1], C)
        Whz, bhz = lin(ks[2], ks[3], C)
        Wxr, bxr = lin(ks[4], ks[5], C)
        Whr, bhr = lin(ks[6], ks[7], C)
        Wxh, bxh = lin(ks[8], ks[9], C)
        Whh, bhh = lin(ks[10], ks[11], C)
        Whq, bhq = lin(ks[12], ks[13], C)
        X = jax.random.normal(ks[14], (B, T, C), jnp.float32)
        h0 = jax.random.normal(ks[15], (B, C), jnp.float32)
        return {'X': X, 'h0': h0, 'Wxz': Wxz, 'bxz': bxz, 'Whz': Whz, 'bhz': bhz, 'Wxr': Wxr, 'bxr': bxr, 'Whr': Whr, 'bhr': bhr, 'Wxh': Wxh, 'bxh': bxh, 'Whh': Whh, 'bhh': bhh, 'Whq': Whq, 'bhq': bhq}
    _L0_cond_all = _L0_cond_setup()
    _L0_cond_in = {k: v for k, v in _L0_cond_all.items() if k in ('Wxz', 'bxz', 'Whz', 'bhz', 'Wxr', 'bxr', 'Whr', 'bhr', 'Wxh', 'bxh', 'Whh', 'bhh', 'Whq', 'bhq')}
    del _L0_cond_all

    def _L0_ffn_setup():
        import math
        import jax, jax.numpy as jnp
        import numpy as np
        B, S, D, H, E, K = (4, 256, 128, 512, 8, 2)
        CAPACITY_RATIO = 1.05
        key = jax.random.key(seed)
        k0, k1, k2, k3 = jax.random.split(key, 4)
        x = jax.random.normal(k0, (B, S, D), jnp.float32)
        Wg = jax.random.normal(k1, (D, E), jnp.float32) * 0.02
        W1 = jax.random.normal(k2, (E, D, H), jnp.float32) * 0.02
        b1 = jnp.zeros((E, H), jnp.float32)
        W2 = jax.random.normal(k3, (E, H, D), jnp.float32) * 0.02
        b2 = jnp.zeros((E, D), jnp.float32)
        return {'x': x, 'Wg': Wg, 'W1': W1, 'b1': b1, 'W2': W2, 'b2': b2}
    _L0_ffn_all = _L0_ffn_setup()
    _L0_ffn_in = {k: v for k, v in _L0_ffn_all.items() if k in ('Wg', 'W1', 'b1', 'W2', 'b2')}
    del _L0_ffn_all

    def _L1_cond_setup():
        import jax, jax.numpy as jnp
        import numpy as np
        key = jax.random.key(seed)
        ks = jax.random.split(key, 8)
        B, L, D, N, K = (4, 512, 128, 64, 4)
        return {'x': jax.random.normal(ks[0], (B, L, D), dtype=jnp.float32), 'conv_w': jax.random.normal(ks[1], (K, 1, D), dtype=jnp.float32) * 0.1, 'conv_b': jnp.zeros((D,), dtype=jnp.float32), 'Wp': jax.random.normal(ks[2], (D, 2 * N), dtype=jnp.float32) * (1.0 / np.sqrt(D)), 'bp': jnp.zeros((2 * N,), dtype=jnp.float32), 'Ws': jax.random.normal(ks[3], (D, N), dtype=jnp.float32) * (1.0 / np.sqrt(D)), 'bs': jnp.zeros((N,), dtype=jnp.float32), 'A_log': jax.random.normal(ks[4], (N,), dtype=jnp.float32) * 0.02, 'dt_log': jax.random.normal(ks[5], (N,), dtype=jnp.float32) * 0.02, 'Wo': jax.random.normal(ks[6], (N, D), dtype=jnp.float32) * (1.0 / np.sqrt(N)), 'bo': jnp.zeros((D,), dtype=jnp.float32)}
    _L1_cond_all = _L1_cond_setup()
    _L1_cond_in = {k: v for k, v in _L1_cond_all.items() if k in ('conv_b', 'Wp', 'bp', 'Ws', 'bs', 'A_log', 'dt_log', 'Wo', 'bo')}
    del _L1_cond_all

    def _L1_ffn_setup():
        import jax, jax.numpy as jnp
        import numpy as np
        B, T, C, I, E = (4, 256, 128, 352, 7)

        def _swiglu(h, w1, w2, w3):
            return jax.nn.silu(h @ w1.T) * (h @ w3.T) @ w2.T
        key = jax.random.key(seed)
        ks = jax.random.split(key, 9)
        sc_c = 1.0 / np.sqrt(C)
        sc_i = 1.0 / np.sqrt(I)
        return {'x': jax.random.normal(ks[0], (B, T, C), jnp.float32), 'router_w': jax.random.normal(ks[1], (E, C), jnp.float32) * sc_c, 'routing_bias': jnp.zeros((E,), jnp.float32), 'sw1': jax.random.normal(ks[2], (I, C), jnp.float32) * sc_c, 'sw2': jax.random.normal(ks[3], (C, I), jnp.float32) * sc_i, 'sw3': jax.random.normal(ks[4], (I, C), jnp.float32) * sc_c, 'ew1': jax.random.normal(ks[5], (E, I, C), jnp.float32) * sc_c, 'ew2': jax.random.normal(ks[6], (E, C, I), jnp.float32) * sc_i, 'ew3': jax.random.normal(ks[7], (E, I, C), jnp.float32) * sc_c}
    _L1_ffn_all = _L1_ffn_setup()
    _L1_ffn_in = {k: v for k, v in _L1_ffn_all.items() if k in ('router_w', 'routing_bias', 'sw1', 'sw2', 'sw3', 'ew1', 'ew2', 'ew3')}
    del _L1_ffn_all
    return {'x': x, 'cond_1024': cond_1024, 'L0_cond_Wxz': _L0_cond_in['Wxz'], 'L0_cond_bxz': _L0_cond_in['bxz'], 'L0_cond_Whz': _L0_cond_in['Whz'], 'L0_cond_bhz': _L0_cond_in['bhz'], 'L0_cond_Wxr': _L0_cond_in['Wxr'], 'L0_cond_bxr': _L0_cond_in['bxr'], 'L0_cond_Whr': _L0_cond_in['Whr'], 'L0_cond_bhr': _L0_cond_in['bhr'], 'L0_cond_Wxh': _L0_cond_in['Wxh'], 'L0_cond_bxh': _L0_cond_in['bxh'], 'L0_cond_Whh': _L0_cond_in['Whh'], 'L0_cond_bhh': _L0_cond_in['bhh'], 'L0_cond_Whq': _L0_cond_in['Whq'], 'L0_cond_bhq': _L0_cond_in['bhq'], 'L0_ffn_Wg': _L0_ffn_in['Wg'], 'L0_ffn_W1': _L0_ffn_in['W1'], 'L0_ffn_b1': _L0_ffn_in['b1'], 'L0_ffn_W2': _L0_ffn_in['W2'], 'L0_ffn_b2': _L0_ffn_in['b2'], 'L1_cond_conv_b': _L1_cond_in['conv_b'], 'L1_cond_Wp': _L1_cond_in['Wp'], 'L1_cond_bp': _L1_cond_in['bp'], 'L1_cond_Ws': _L1_cond_in['Ws'], 'L1_cond_bs': _L1_cond_in['bs'], 'L1_cond_A_log': _L1_cond_in['A_log'], 'L1_cond_dt_log': _L1_cond_in['dt_log'], 'L1_cond_Wo': _L1_cond_in['Wo'], 'L1_cond_bo': _L1_cond_in['bo'], 'L1_ffn_router_w': _L1_ffn_in['router_w'], 'L1_ffn_routing_bias': _L1_ffn_in['routing_bias'], 'L1_ffn_sw1': _L1_ffn_in['sw1'], 'L1_ffn_sw2': _L1_ffn_in['sw2'], 'L1_ffn_sw3': _L1_ffn_in['sw3'], 'L1_ffn_ew1': _L1_ffn_in['ew1'], 'L1_ffn_ew2': _L1_ffn_in['ew2'], 'L1_ffn_ew3': _L1_ffn_in['ew3']}

def reference(x, cond_1024, L0_cond_Wxz, L0_cond_bxz, L0_cond_Whz, L0_cond_bhz, L0_cond_Wxr, L0_cond_bxr, L0_cond_Whr, L0_cond_bhr, L0_cond_Wxh, L0_cond_bxh, L0_cond_Whh, L0_cond_bhh, L0_cond_Whq, L0_cond_bhq, L0_ffn_Wg, L0_ffn_W1, L0_ffn_b1, L0_ffn_W2, L0_ffn_b2, L1_cond_conv_b, L1_cond_Wp, L1_cond_bp, L1_cond_Ws, L1_cond_bs, L1_cond_A_log, L1_cond_dt_log, L1_cond_Wo, L1_cond_bo, L1_ffn_router_w, L1_ffn_routing_bias, L1_ffn_sw1, L1_ffn_sw2, L1_ffn_sw3, L1_ffn_ew1, L1_ffn_ew2, L1_ffn_ew3):
    import jax
    import jax.numpy as jnp

    def _L0_cond_ref(X, h0, Wxz, bxz, Whz, bhz, Wxr, bxr, Whr, bhr, Wxh, bxh, Whh, bhh, Whq, bhq):
        import jax, jax.numpy as jnp
        import numpy as np
        B, T, C = (64, 64, 128)
        Xz = jnp.einsum('btc,hc->tbh', X, Wxz) + bxz
        Xr = jnp.einsum('btc,hc->tbh', X, Wxr) + bxr
        Xh = jnp.einsum('btc,hc->tbh', X, Wxh) + bxh

        def step(H, xs):
            xz, xr, xh = xs
            Z = jax.nn.sigmoid(xz + H @ Whz.T + bhz)
            R = jax.nn.sigmoid(xr + H @ Whr.T + bhr)
            H_tilda = jnp.tanh(xh + R * H @ Whh.T + bhh)
            H_new = Z * H + (1.0 - Z) * H_tilda
            Y = H_new @ Whq.T + bhq
            return (H_new, Y)
        _, Ys = jax.lax.scan(step, h0, (Xz, Xr, Xh))
        return jnp.transpose(Ys, (1, 0, 2))

    def _L0_ffn_ref(x, Wg, W1, b1, W2, b2):
        import math
        import jax, jax.numpy as jnp
        import numpy as np
        B, S, D, H, E, K = (4, 256, 128, 512, 8, 2)
        CAPACITY_RATIO = 1.05
        b, s, d = x.shape
        e = Wg.shape[1]
        n = b * s
        cap = int(math.ceil(n * K / e * CAPACITY_RATIO))
        xf = x.reshape(n, d)
        probs = jax.nn.softmax(xf @ Wg, axis=-1)
        topv, topi = jax.lax.top_k(probs, K)
        gates = topv / jnp.sum(topv, axis=-1, keepdims=True)
        eidx = topi.reshape(-1)
        oh = jax.nn.one_hot(eidx, e, dtype=jnp.int32)
        pos = jnp.sum(jnp.cumsum(oh, axis=0) * oh, axis=-1) - 1
        keep = pos < cap
        dest = jnp.where(keep, eidx * cap + pos, e * cap)
        xr = jnp.repeat(xf, K, axis=0)
        buf = jnp.zeros((e * cap + 1, d), x.dtype).at[dest].set(xr)
        expert_in = buf[:e * cap].reshape(e, cap, d)
        h = jax.nn.gelu(jnp.einsum('ecd,edh->ech', expert_in, W1) + b1[:, None, :])
        y = jnp.einsum('ech,ehd->ecd', h, W2) + b2[:, None, :]
        yf = jnp.concatenate([y.reshape(e * cap, d), jnp.zeros((1, d), y.dtype)], axis=0)
        gathered = yf[dest]
        w = (gates.reshape(-1) * keep.astype(gates.dtype))[:, None]
        out = (gathered * w).reshape(n, K, d).sum(axis=1).reshape(b, s, d)
        return out

    def _L1_cond_ref(x, conv_w, conv_b, Wp, bp, Ws, bs, A_log, dt_log, Wo, bo):
        import jax, jax.numpy as jnp
        import numpy as np
        B, L, D = x.shape
        K = conv_w.shape[0]
        N = Ws.shape[1]
        x_pad = jnp.pad(x, ((0, 0), (K - 1, 0), (0, 0)))
        conv = conv_b + sum((x_pad[:, k:k + L, :] * conv_w[k, 0] for k in range(K)))
        proj = conv @ Wp + bp
        B_t = jax.nn.softplus(proj[..., :N])
        C_t = jnp.tanh(proj[..., N:])
        u = x @ Ws + bs
        A = -jax.nn.softplus(A_log)
        dt = jax.nn.softplus(dt_log)
        decay = 1.0 + dt * A

        def step(state, inputs):
            u_t, b_t, c_t = inputs
            state = decay * state + dt * b_t * u_t
            return (state, c_t * state)
        init = jnp.zeros((B, N), dtype=x.dtype)
        xs = tuple((jnp.swapaxes(a, 0, 1) for a in (u, B_t, C_t)))
        _, ys = jax.lax.scan(step, init, xs, unroll=4)
        y = jnp.swapaxes(ys, 0, 1)
        return y @ Wo + bo

    def _L1_ffn_ref(x, router_w, routing_bias, sw1, sw2, sw3, ew1, ew2, ew3):
        import jax, jax.numpy as jnp
        import numpy as np
        B, T, C, I, E = (4, 256, 128, 352, 7)

        def _swiglu(h, w1, w2, w3):
            return jax.nn.silu(h @ w1.T) * (h @ w3.T) @ w2.T
        b, t, c = x.shape
        shared_out = _swiglu(x, sw1, sw2, sw3)
        logits = jnp.clip(x @ router_w.T + routing_bias, -50.0, 50.0)
        probs = jax.nn.sigmoid(logits)
        num_switched = 1
        topk_probs, topk_idx = jax.lax.top_k(probs, num_switched)
        topk_probs = jnp.clip(topk_probs, 1e-08, 1.0 - 1e-08)
        xf = x.reshape(-1, c)
        sel = topk_idx.reshape(-1)
        p = topk_probs.reshape(-1)
        switched = jnp.zeros_like(xf)
        n_experts = ew1.shape[0]
        for e in range(n_experts):
            y = _swiglu(xf, ew1[e], ew2[e], ew3[e])
            w = jnp.where(sel == e, p, 0.0)
            switched = switched + w[:, None] * y
        switched = switched.reshape(b, t, c)
        total_weight = 0.5 + topk_probs.sum(axis=-1)
        total_weight = jnp.clip(total_weight[..., None] + 1e-08, 0.5, 2.0)
        return 0.5 / total_weight * shared_out + switched / total_weight
    x = x + _L0_ffn_ref(_L0_cond_ref(x, cond_1024, L0_cond_Wxz, L0_cond_bxz, L0_cond_Whz, L0_cond_bhz, L0_cond_Wxr, L0_cond_bxr, L0_cond_Whr, L0_cond_bhr, L0_cond_Wxh, L0_cond_bxh, L0_cond_Whh, L0_cond_bhh, L0_cond_Whq, L0_cond_bhq), L0_ffn_Wg, L0_ffn_W1, L0_ffn_b1, L0_ffn_W2, L0_ffn_b2)
    x = x + _L1_ffn_ref(_L1_cond_ref(x, cond_1024[:, None, :], L1_cond_conv_b, L1_cond_Wp, L1_cond_bp, L1_cond_Ws, L1_cond_bs, L1_cond_A_log, L1_cond_dt_log, L1_cond_Wo, L1_cond_bo), L1_ffn_router_w, L1_ffn_routing_bias, L1_ffn_sw1, L1_ffn_sw2, L1_ffn_sw3, L1_ffn_ew1, L1_ffn_ew2, L1_ffn_ew3)
    return x

_drawn_inputs = setup_inputs


def setup_inputs(seed=0):
    import zlib

    import numpy as np

    out = dict(_drawn_inputs(seed))
    spreads = {'L0_ffn_b1': (0.0, 0.1),
     'L0_ffn_b2': (0.0, 0.1),
     'L1_cond_conv_b': (0.0, 0.1),
     'L1_cond_bp': (0.0, 0.1),
     'L1_cond_bs': (0.0, 0.1),
     'L1_cond_bo': (0.0, 0.1),
     'L1_ffn_routing_bias': (0.0, 0.1)}
    factors = {'L0_cond_bhr': 3.468, 'L0_cond_bxr': 8.0}
    for name, (base, spread) in spreads.items():
        noise = np.random.default_rng([zlib.crc32(name.encode()), seed]).standard_normal(out[name].shape)
        drawn = base * np.exp(spread * noise) if base else spread * noise
        out[name] = jnp.asarray(drawn.astype(out[name].dtype))
    for name, factor in factors.items():
        out[name] = (out[name] * factor).astype(out[name].dtype)
    return out
```

```python
from contextlib import ExitStack

import concourse.bass as bass
from concourse import mybir

F32 = mybir.dt.float32
BF16 = mybir.dt.bfloat16
U32 = mybir.dt.uint32
ALU = mybir.AluOpType
ACT = mybir.ActivationFunctionType
AX_X = mybir.AxisListType.X

P = 128
B, T, D = 4, 256, 128
STEPS = 32
BLOCKS = T // STEPS
SLOTS = BLOCKS + 2
E0, H0 = 8, 512
HC = H0 // P
CAP = 269
NS = 64
KCONV = 4
E1, I1 = 8, 352
IC = (128, 128, 96)
TILES = B * T // P
GRP = 512
MPG = GRP // P


def adaln_ffn_kernel(nc, a, out):
    with ExitStack() as ctx:
        def sb(name, shape, dt=F32):
            return ctx.enter_context(nc.sbuf_tensor(name, shape, dt))

        def psum(name):
            return ctx.enter_context(nc.psum_tensor(name, [P, 512], F32))

        def sem(name):
            return ctx.enter_context(nc.semaphore(name))

        x_sb = sb("x_sb", [P, (BLOCKS + 1) * P])
        gw = sb("gw", [P, 7, P])
        gbias = sb("gbias", [P, 3, 2])
        qbias = sb("qbias", [P, 1])
        h0 = sb("h0", [P, B])
        consts = sb("consts", [P, 4, P])
        iota8 = sb("iota8", [P, 8])
        wg = sb("wg", [P, E0])
        w1 = sb("w1", [P, E0, H0])
        b1 = sb("b1", [P, E0, HC])
        w2 = sb("w2", [P, E0, HC, D])
        b2 = sb("b2", [1, E0, D])
        ident, m_before, m_same, m_below = (consts[:, k, :] for k in range(4))

        gws = sb("gws", [P, 5, P])
        wr_q, wr_p, wz_g, wh_rh, wq_g = (gws[:, k, :] for k in range(5))
        gb = sb("gb", [P, 3])
        xp = sb("xp", [P, 3, P])
        G = sb("G", [P, B, STEPS])
        Q4 = sb("Q4", [P, B])
        P2 = sb("P2", [P, B])
        RH4 = sb("RH4", [P, B])
        tr = sb("tr", [P, B])
        tz = sb("tz", [P, B])
        ht = sb("ht", [P, B])
        yT = sb("yT", [P, P])
        hT = [sb("hT%d" % k, [P, HC, P]) for k in range(2)]
        ones_row = sb("ones_row", [1, P])
        warm = sb("warm", [P, 256], BF16)
        lg = sb("lg", [P, E0])
        top8 = sb("top8", [P, 8])
        idx8 = sb("idx8", [P, 8], U32)
        idxf = sb("idxf", [P, 2])
        gap = sb("gap", [P, 1])
        tgap = sb("tgap", [P, 1])
        gate = [sb("gate%d" % k, [P, SLOTS]) for k in range(2)]
        oh = [sb("oh%d" % k, [P, SLOTS, E0]) for k in range(2)]
        cnt = sb("cnt", [P, SLOTS, E0])
        A = [sb("A%d" % k, [P, SLOTS, D]) for k in range(2)]

        pref = sb("pref", [P, SLOTS + 1, E0])
        kept = sb("kept", [P, BLOCKS, E0])
        kd = sb("kd", [P, BLOCKS, E0])
        kg = [sb("kg%d" % k, [P, BLOCKS]) for k in range(2)]
        diag = [sb("diag%d" % k, [P, 2, P]) for k in range(2)]
        x1p = sb("x1p", [P, B, KCONV - 1 + T])

        wp = sb("wp", [P, 2 * NS])
        ws = sb("ws", [P, NS])
        wo = sb("wo", [NS, D])
        cb = sb("cb", [P, 1])
        bpb = sb("bpb", [NS, 2])
        bs = sb("bs", [NS, 1])
        bo = sb("bo", [P, 1])
        alog = sb("alog", [NS, 2])
        sp_t = sb("sp_t", [NS, 2])
        sp_r = sb("sp_r", [NS, 2])
        sp_v = sb("sp_v", [NS, 2])
        decay = sb("decay", [NS, 1])
        decay_row = sb("decay_row", [NS, T])
        conv = sb("conv", [P, B, T])
        Cg = sb("Cg", [NS, B * T])
        Bg = sb("Bg", [NS, B * T])
        Bt = sb("Bt", [NS, B * T])
        U = sb("U", [NS, B * T])
        S = sb("S", [NS, B * T])
        xc = sb("xc", [P, B * T])

        rw = sb("rw", [P, 7])
        rb = sb("rb", [1, 7])
        v1 = sb("v1", [P, E1, I1])
        v3 = sb("v3", [P, E1, I1])
        v2a = sb("v2a", [P, E1, 2, D])
        v2b = sb("v2b", [IC[2], E1, D])
        prob = sb("prob", [P, TILES, 8])
        pr_e = sb("pr_e", [P, TILES, 7])
        ptop = sb("ptop", [P, TILES, 8])
        pidx = sb("pidx", [P, TILES, 8], U32)
        pidf = sb("pidf", [P, TILES])
        pw = sb("pw", [P, TILES])
        ptw = sb("ptw", [P, TILES])
        prt = sb("prt", [P, TILES])
        psel = sb("psel", [P, TILES])
        wt = sb("wt", [P, TILES, 8])
        sg = sb("sg", [P, 2, GRP])
        hh = sb("hh", [P, 2, 3, GRP])
        acc = sb("acc", [P, TILES, D])

        bank = [psum("bank%d" % k) for k in range(8)]
        pre = [bank[g][:, 0:P].rearrange("p (b t) -> p b t", b=B) for g in range(3)]
        ps_h = [bank[3 + k][:, :].rearrange("p (c t) -> p c t", c=HC) for k in range(2)]
        ps_y = bank[5][:, 0:D]
        ps_misc = bank[6]
        ps_warm = bank[7][:, 0:256]

        in_gru, in_moe, in_rec, in_l1 = sem("in_gru"), sem("in_moe"), sem("in_rec"), sem("in_l1")
        pool_set = sem("pool_set")
        weights_scaled, gbias_sum = sem("weights_scaled"), sem("gbias_sum")
        xp_ps, xp_done, xp_used = sem("xp_ps"), sem("xp_done"), sem("xp_used")
        r_pre, z_pre, h_pre = sem("r_pre"), sem("z_pre"), sem("h_pre")
        r_act, z_act, h_act = sem("r_act"), sem("z_act"), sem("h_act")
        rh_rdy, q_rdy, p_rdy, g_rdy = sem("rh_rdy"), sem("q_rdy"), sem("p_rdy"), sem("g_rdy")
        yt_ps, yt_done, lg_ps, route, gap_act = sem("yt_ps"), sem("yt_done"), sem("lg_ps"), sem("route"), sem("gap_act")
        up_ps, gelu_done, down_ps, acc_done = sem("up_ps"), sem("gelu_done"), sem("down_ps"), sem("acc_done")
        pref_done, pos_ps, keep_done = sem("pref_done"), sem("pos_ps"), sem("keep_done")
        diag_done, x1_ps, x1_done = sem("diag_done"), sem("x1_ps"), sem("x1_done")
        dec_act, dec_dve = sem("dec_act"), sem("dec_dve")
        conv_done, cproj_ps, bproj_ps, u_ps = sem("conv_done"), sem("cproj_ps"), sem("bproj_ps"), sem("u_ps")
        sp_act, c_act, rec = sem("sp_act"), sem("c_act"), sem("rec")
        xc_ps, xc_done = sem("xc_ps"), sem("xc_done")
        rl_ps, rt, e_act = sem("rl_ps"), sem("rt"), sem("e_act")
        res_ps, res_done = sem("res_ps"), sem("res_done")
        g1_ps, g3_ps, silu_done, hh_done, out_ps, acc2 = (sem("g1_ps"), sem("g3_ps"), sem("silu_done"),
                                                         sem("hh_done"), sem("out_ps"), sem("acc2"))
        stored = sem("stored")

        def up_cnt(s, e):
            return 8 * (s - 1) + e + 2

        def gelu_cnt(s, e):
            return 8 * (s - 1) + e + 3

        def down_cnt(s, e):
            return 8 * (s - 1) + e + 4

        N_ROUTE = 6
        N_GRU_IN, N_MOE_IN, N_REC_IN, N_L1_IN = 7, 6, 8, 6

        block = ctx.enter_context(nc.Block())

        @block.sync
        def _(sp):
            for dst, src in ((x_sb[:, 0:BLOCKS * P], "xT"), (gw[:, :, :], "gw"), (gbias[:, :, :], "gbias"),
                             (qbias[:, :], "qbias"), (h0[:, :], "h0"), (consts[:, :, :], "consts"),
                             (alog[:, :], "alog")):
                sp.dma_start(dst, a[src]).then_inc(in_gru, 16)
            for dst, src in ((wg[:, :], "wg"), (w1[:, :, :], "w1"), (b1[:, :, :], "b1"), (w2[:, :, :, :], "w2"),
                             (b2[:, :, :], "b2"), (iota8[:, :], "iota8")):
                sp.dma_start(dst, a[src]).then_inc(in_moe, 16)
            for dst, src in ((wp[:, :], "wp"), (ws[:, :], "ws"), (wo[:, :], "wo"), (cb[:, :], "cb"),
                             (bpb[:, :], "bpb"), (bs[:, :], "bs"), (bo[:, :], "bo"), (rw[:, :], "rw")):
                sp.dma_start(dst, a[src]).then_inc(in_rec, 16)
            for dst, src in ((rb[:, :], "rb"), (v1[:, :, :], "v1"), (v3[:, :, :], "v3"),
                             (v2a[:, :, :, :], "v2a"), (v2b[:, :, :], "v2b")):
                sp.dma_start(dst, a[src]).then_inc(in_l1, 16)
            for g in range(2):
                sp.wait_ge(acc2, E1 * MPG * (g + 1))
                sp.dma_start(out[g * GRP:(g + 1) * GRP, :].rearrange("(m p) d -> p m d", p=P),
                             acc[:, g * MPG:(g + 1) * MPG, :]).then_inc(stored, 16)
            sp.wait_ge(stored, 32)

        @block.gpsimd
        def _(pool):
            nc.gpsimd.memset(x_sb[:, BLOCKS * P:], 0.0)
            nc.gpsimd.memset(ones_row[:, :], 1.0)
            nc.gpsimd.memset(warm[:, :], 1.0)
            nc.gpsimd.memset(x1p[:, :, 0:KCONV - 1], 0.0)
            nc.gpsimd.memset(hT[0][:, :, :], 0.0)
            nc.gpsimd.memset(hT[1][:, :, :], 0.0).then_inc(gelu_done, 1)
            nc.gpsimd.memset(oh[0][:, 0, :], 0.0)
            nc.gpsimd.memset(oh[1][:, 0, :], 0.0)
            nc.gpsimd.memset(A[0][:, 0, :], 0.0)
            nc.gpsimd.memset(A[1][:, 0, :], 0.0).then_inc(down_ps, 1)
            nc.gpsimd.memset(prob[:, :, :], -1.0)
            nc.gpsimd.memset(pref[:, 0:3, :], 0.0).then_inc(pool_set, 1)

        @block.tensor
        def _(pe):
            def mm(o, lhsT, rhs, start=False, stop=False):
                return nc.tensor.matmul(o, lhsT, rhs, start=start, stop=stop, skip_group_check=True)

            def keep_warm(n):
                mm(ps_warm[:, 0:n], warm[:, 0:P], warm[:, 0:n], start=True, stop=True)

            def x_products(i):
                for g in range(3):
                    last = mm(ps_misc[:, g * P:(g + 1) * P], gw[:, g, :], x_sb[:, bass.ds(i * P, P)],
                              start=(g == 0), stop=True)
                last.then_inc(xp_ps, 1)

            def inject(g):
                return mm(bank[g][:, 0:P], ident, xp[:, g, :], start=True)

            def y_product(i):
                pe.wait_ge(g_rdy, i * STEPS + 1)
                mm(ps_misc[:, 0:P], wq_g, G[:, :, :].rearrange("p b t -> p (b t)"), start=True, stop=True)\
                    .then_inc(yt_ps, 1)

            def router_product(i):
                pe.wait_ge(yt_done, i + 1)
                mm(ps_misc[:, 0:E0], yT[:, :], wg[:, :], start=True, stop=True).then_inc(lg_ps, 1)

            def up(s, e, c):
                if c == 0:
                    pe.wait_ge(gelu_done, gelu_cnt(s, e - 2))
                    if e == 0:
                        pe.wait_ge(yt_done, s)
                m = mm(ps_h[e % 2][:, c, :], w1[:, e, c * P:(c + 1) * P], yT[:, :], start=(c == 0), stop=True)
                if c == HC - 1:
                    m.then_inc(up_ps, 1)

            def down(s, e, c):
                if c == 0:
                    pe.wait_ge(gelu_done, gelu_cnt(s, e))
                    pe.wait_ge(acc_done, down_cnt(s, e - 1))
                m = mm(ps_y, hT[e % 2][:, c, :], w2[:, e, c, :], start=(c == 0))
                if c == HC - 1:
                    mm(ps_y, ones_row[:, :], b2[:, e, :], stop=True).then_inc(down_ps, 1)

            def side(i, t, half):
                if t % 4 in (2, 3):
                    for c in ((t % 4 - 2) * 2 + half,):
                        up(i + 1, t // 4, c)
                else:
                    e = t // 4 - 2
                    s = i + 1 if e >= 0 else i
                    down(s, e % E0, (t % 4) * 2 + half)
                if (t, half) == (0, 1):
                    y_product(i)
                if (t, half) == (1, 1):
                    router_product(i)
                if (t, half) == (8, 1):
                    pe.wait_ge(route, N_ROUTE * i + 1)
                    x_products(i + 1)
                if (t, half) == (31, 1):
                    pe.wait_ge(xp_done, i + 2)
                    inject(0)

            pe.wait_ge(in_gru, 16 * N_GRU_IN)
            pe.wait_ge(pool_set, 1)
            x_products(0)
            pe.wait_ge(xp_done, 1)
            inject(0)
            pe.wait_ge(weights_scaled, 5)
            pe.wait_ge(in_moe, 16 * N_MOE_IN)
            with pe.Fori(0, BLOCKS) as i:
                for t in range(STEPS):
                    n = i * STEPS + t
                    pe.wait_ge(q_rdy, n + 1)
                    mm(pre[0][:, :, t], wr_q, Q4[:, :])
                    pe.wait_ge(p_rdy, n + 1)
                    mm(pre[0][:, :, t], wr_p, P2[:, :]).then_inc(r_pre, 1)
                    if t == 0:
                        inject(1)
                    else:
                        side(i, t, 0)
                    pe.wait_ge(g_rdy, n + 1)
                    mm(pre[1][:, :, t], wz_g, G[:, :, (t - 1) % STEPS]).then_inc(z_pre, 1)
                    if t == 0:
                        inject(2).then_inc(xp_used, 1)
                    keep_warm(256)
                    pe.wait_ge(rh_rdy, n + 1)
                    mm(pre[2][:, :, t], wh_rh, RH4[:, :], stop=True).then_inc(h_pre, 1)
                    if t == 0:
                        side(i, 0, 0)
                    side(i, t, 1)
                    keep_warm(256)

            y_product(BLOCKS)
            for c in range(HC):
                down(BLOCKS, 6, c)
            router_product(BLOCKS)
            for c in range(HC):
                down(BLOCKS, 7, c)
            for e in range(E0 + 2):
                if e < E0:
                    for c in range(HC):
                        up(SLOTS - 1, e, c)
                if e >= 2:
                    for c in range(HC):
                        down(SLOTS - 1, e - 2, c)
                if e == 4:
                    pe.wait_ge(pref_done, BLOCKS)
                    mm(ps_misc[:, 0:BLOCKS * E0], m_before, cnt[:, 2:, :], start=True)
                    mm(ps_misc[:, 0:BLOCKS * E0], m_same, pref[:, 2:SLOTS, :])
                    for k in range(BLOCKS):
                        last = mm(ps_misc[:, k * E0:(k + 1) * E0], m_below, pref[:, SLOTS, :], stop=True)
                    last.then_inc(pos_ps, 1)

            for k in range(BLOCKS):
                pe.wait_ge(diag_done, 2 * k + 2)
                if k >= 2:
                    pe.wait_ge(x1_done, k - 1)
                if k == BLOCKS - 1:
                    pe.wait_ge(acc_done, down_cnt(SLOTS - 1, E0 - 1))
                o = bank[k % 2][:, 0:P]
                mm(o, A[0][:, k + 2, :], diag[0][:, k % 2, :], start=True)
                mm(o, A[1][:, k + 2, :], diag[1][:, k % 2, :], stop=True).then_inc(x1_ps, 1)

            pe.wait_ge(in_rec, 16 * N_REC_IN)
            pe.wait_ge(conv_done, 1)
            xg = [x1p[:, 2 * g:2 * g + 2, KCONV - 1:] for g in range(2)]
            for g in range(2):
                mm(bank[2 + g][0:NS, :], wp[:, NS:], conv[:, 2 * g:2 * g + 2, :], start=True, stop=True).then_inc(cproj_ps, 1)
            for g in range(2):
                mm(bank[4 + g][0:NS, :], wp[:, 0:NS], conv[:, 2 * g:2 * g + 2, :], start=True, stop=True).then_inc(bproj_ps, 1)
            pe.wait_ge(x1_done, BLOCKS)
            for g in range(2):
                mm(bank[g][0:NS, :], ws[:, :], xg[g], start=True, stop=True).then_inc(u_ps, 1)
            pe.wait_ge(in_l1, 16 * (N_L1_IN - 1))
            for m in range(TILES):
                b, h = m // 2, m % 2
                last = mm(bank[6 + m // 4][:, (m % 4) * P:(m % 4 + 1) * P],
                          x1p[:, b, KCONV - 1 + h * P:KCONV - 1 + (h + 1) * P], ident, start=(m % 4 == 0), stop=True)
            last.then_inc(res_ps, 1)
            for g in range(2):
                pe.wait_ge(rec, 8 + 4 * g + 4)
                pe.wait_ge(c_act, 2)
                mm(bank[2 + g][:, :], wo[:, :], Bg[:, g * GRP:(g + 1) * GRP], start=True, stop=True).then_inc(xc_ps, 1)
            pe.wait_ge(xc_done, 2)
            for m in range(TILES):
                o = bank[4][:, m * 7:(m + 1) * 7]
                mm(o, xc[:, m * P:(m + 1) * P], rw[:, :], start=(m == 0))
                last = mm(o, ones_row[:, :], rb[:, :], stop=True)
            last.then_inc(rl_ps, 1)

            def ups(g, e, c):
                k = (g * E1 + e) * 3 + c
                n = IC[c]
                cols = slice(c * P, c * P + n)
                rhs = xc[:, g * GRP:(g + 1) * GRP]
                if k >= 2:
                    pe.wait_ge(hh_done, k - 1)
                if k < 1:
                    pe.wait_ge(xc_done, 2)
                mm(bank[k % 2 * 2][0:n, :], v1[:, e, cols], rhs, start=True, stop=True).then_inc(g1_ps, 1)
                mm(bank[k % 2 * 2 + 1][0:n, :], v3[:, e, cols], rhs, start=True, stop=True).then_inc(g3_ps, 1)

            def outs(g, e):
                q = g * E1 + e
                pe.wait_ge(hh_done, 3 * q + 3)
                if q < 2:
                    pe.wait_ge(res_done, 2)
                else:
                    pe.wait_ge(acc2, MPG * (q - 1))
                for m in range(MPG):
                    o = bank[6 + q % 2][:, m * P:(m + 1) * P]
                    for c in range(3):
                        w = v2a[:, e, c, :] if c < 2 else v2b[:, e, :]
                        last = mm(o, hh[0:IC[c], q % 2, c, m * P:(m + 1) * P], w,
                                  start=(m == 0 and c == 0), stop=(c == 2))
                last.then_inc(out_ps, 1)

            for q in range(2 * E1 + 1):
                if q < 2 * E1:
                    for c in range(3):
                        ups(q // E1, q % E1, c)
                if q >= 1:
                    outs((q - 1) // E1, (q - 1) % E1)

        @block.scalar
        def _(act):
            nc.scalar.preload_act_table_set("natural_log_exp_and_others")
            act.wait_ge(in_gru, 16 * N_GRU_IN)
            nc.scalar.activation(sp_t[:, :], alog[:, :], ACT.Abs).then_inc(dec_act, 1)
            act.wait_ge(dec_act, 1)
            nc.scalar.activation(sp_t[:, :], sp_t[:, :], ACT.Exp, scale=-1.0).then_inc(dec_act, 1)
            act.wait_ge(dec_act, 2)
            nc.scalar.activation(sp_t[:, :], sp_t[:, :], ACT.Ln, bias=1.0).then_inc(dec_act, 1)
            nc.scalar.activation(sp_r[:, :], alog[:, :], ACT.Relu).then_inc(dec_act, 1)
            nc.scalar.preload_act_table_set("gelu_apprx_tanh_and_others")

            def xp_evac(g):
                o = nc.scalar.activation(xp[:, g, :], ps_misc[:, g * P:(g + 1) * P], ACT.Identity,
                                         bias=gb[:, g:g + 1])
                if g == 2:
                    o.then_inc(xp_done, 1)

            def gelu(s, e, c):
                if c == 0:
                    act.wait_ge(up_ps, up_cnt(s, e))
                    act.wait_ge(down_ps, down_cnt(s, e - 2))
                g = nc.scalar.activation(hT[e % 2][:, c, :], ps_h[e % 2][:, c, :], ACT.Gelu_apprx_tanh,
                                         bias=b1[:, e, c:c + 1])
                if c == HC - 1:
                    g.then_inc(gelu_done, 1)

            def gap_tanh(i):
                act.wait_ge(route, N_ROUTE * i + 2)
                nc.scalar.activation(tgap[:, :], gap[:, :], ACT.Tanh, scale=0.5).then_inc(gap_act, 1)

            act.wait_ge(gbias_sum, 1)
            act.wait_ge(xp_ps, 1)
            for g in range(3):
                xp_evac(g)
            act.wait_ge(in_moe, 16 * N_MOE_IN)
            act.wait_ge(pool_set, 1)
            with act.Fori(0, BLOCKS) as i:
                for t in range(STEPS):
                    n = i * STEPS + t
                    act.wait_ge(r_pre, n + 1)
                    nc.scalar.activation(tr[:, :], pre[0][:, :, t], ACT.Tanh, scale=0.5).then_inc(r_act, 1)
                    e = t // 4 - 1
                    gelu(i + 1 if e >= 0 else i, e % E0, t % 4)
                    act.wait_ge(z_pre, n + 1)
                    nc.scalar.activation(tz[:, :], pre[1][:, :, t], ACT.Tanh, scale=0.5).then_inc(z_act, 1)
                    act.wait_ge(h_pre, n + 1)
                    nc.scalar.activation(ht[:, :], pre[2][:, :, t], ACT.Tanh).then_inc(h_act, 1)
                    if t == 8:
                        gap_tanh(i)
                    if t in (12, 13, 14):
                        if t == 12:
                            act.wait_ge(xp_ps, i + 2)
                            act.wait_ge(xp_used, i + 1)
                        xp_evac(t - 12)
            for c in range(HC):
                gelu(BLOCKS, 7, c)
            for e in range(E0):
                for c in range(HC):
                    gelu(SLOTS - 1, e, c)
                if e == 0:
                    gap_tanh(BLOCKS)

            act.wait_ge(in_rec, 16 * N_REC_IN)
            for g in range(2):
                act.wait_ge(cproj_ps, g + 1)
                nc.scalar.activation(Cg[:, g * GRP:(g + 1) * GRP], bank[2 + g][0:NS, :], ACT.Tanh,
                                     bias=bpb[:, 1:2]).then_inc(c_act, 1)
            nc.scalar.preload_act_table_set("natural_log_exp_and_others")
            for g in range(2):
                act.wait_ge(bproj_ps, g + 1)
                nc.scalar.activation(Bt[:, g * GRP:(g + 1) * GRP], bank[4 + g][0:NS, :], ACT.Abs,
                                     bias=bpb[:, 0:1]).then_inc(sp_act, 1)
            for g in range(2):
                nc.scalar.activation(Bg[:, g * GRP:(g + 1) * GRP], bank[4 + g][0:NS, :], ACT.Relu,
                                     bias=bpb[:, 0:1]).then_inc(sp_act, 1)
            for g in range(2):
                act.wait_ge(sp_act, 4)
                nc.scalar.activation(Bt[:, g * GRP:(g + 1) * GRP], Bt[:, g * GRP:(g + 1) * GRP], ACT.Exp,
                                     scale=-1.0).then_inc(sp_act, 1)
                act.wait_ge(sp_act, 5 + 2 * g)
                nc.scalar.activation(Bt[:, g * GRP:(g + 1) * GRP], Bt[:, g * GRP:(g + 1) * GRP], ACT.Ln,
                                     bias=1.0).then_inc(sp_act, 1)
            for g in range(2):
                act.wait_ge(xc_ps, g + 1)
                nc.scalar.activation(xc[:, g * GRP:(g + 1) * GRP], bank[2 + g][:, :], ACT.Identity,
                                     bias=bo[:, 0:1]).then_inc(xc_done, 1)
            act.wait_ge(rt, 1)
            nc.scalar.activation(pr_e[:, :, :], pr_e[:, :, :], ACT.Exp, scale=-1.0).then_inc(e_act, 1)
            nc.scalar.preload_act_table_set("silu_and_others")
            for k in range(2 * E1 * 3):
                n = IC[k % 3]
                act.wait_ge(g1_ps, k + 1)
                if k >= 2:
                    act.wait_ge(hh_done, k - 1)
                nc.scalar.activation(sg[0:n, k % 2, :], bank[k % 2 * 2][0:n, :], ACT.Silu).then_inc(silu_done, 1)

        @block.vector
        def _(dve):
            V = nc.vector
            dve.wait_ge(in_gru, 16 * N_GRU_IN)
            V.tensor_tensor(gb[:, :], gbias[:, :, 0], gbias[:, :, 1], ALU.add).then_inc(gbias_sum, 1)
            for k, (src, f) in enumerate(((3, 0.25), (3, -0.5), (4, 0.5), (5, 0.25), (6, 0.5))):
                V.tensor_scalar(gws[:, k, :], gw[:, src, :], f, None, ALU.mult).then_inc(weights_scaled, 1)
            V.memset(bank[4][:, :], 0.0).then_inc(up_ps, 1)
            dve.wait_ge(pool_set, 1)
            V.tensor_scalar(Q4[:, :], h0[:, :], 4.0, None, ALU.mult).then_inc(q_rdy, 1)
            V.memset(P2[:, :], 0.0).then_inc(p_rdy, 1)
            V.memset(G[:, :, :], 0.0).then_inc(acc_done, 1)
            dve.wait_ge(acc_done, 1)
            V.tensor_scalar(G[:, :, STEPS - 1], h0[:, :], 2.0, None, ALU.mult).then_inc(g_rdy, 1)
            dve.wait_ge(dec_act, 4)
            V.tensor_tensor(sp_v[:, :], sp_t[:, :], sp_r[:, :], ALU.add).then_inc(dec_dve, 1)
            dve.wait_ge(dec_dve, 1)
            V.tensor_tensor(decay[:, :], sp_v[:, 0:1], sp_v[:, 1:2], ALU.mult).then_inc(dec_dve, 1)
            dve.wait_ge(dec_dve, 2)
            V.tensor_scalar(decay[:, :], decay[:, :], -1.0, 1.0, ALU.mult, ALU.add).then_inc(dec_dve, 1)
            dve.wait_ge(dec_dve, 3)
            V.tensor_copy(decay_row[:, :], decay[:, 0:1].to_broadcast([NS, T])).then_inc(dec_dve, 1)
            dve.wait_ge(in_moe, 16 * N_MOE_IN)

            def yt_evac(i):
                dve.wait_ge(yt_ps, i + 1)
                dve.wait_ge(up_ps, 8 * i + 1)
                V.tensor_scalar(yT[:, :], ps_misc[:, 0:P], qbias[:, 0:1], None, ALU.add).then_inc(yt_done, 1)

            def route_step(i, k):
                s = i + 1
                if k == 0:
                    dve.wait_ge(lg_ps, i + 1)
                    V.tensor_copy(lg[:, :], ps_misc[:, 0:E0])
                    o = V.max(out=top8[:, :], in_=ps_misc[:, 0:E0])
                else:
                    dve.wait_ge(route, N_ROUTE * i + k)
                if k == 1:
                    V.tensor_tensor(gap[:, :], top8[:, 0:1], top8[:, 1:2], ALU.subtract)
                    o = V.max_index(out=idx8[:, :], in_max=top8[:, :], in_values=lg[:, :])
                if k == 2:
                    o = V.tensor_copy(idxf[:, :], idx8[:, 0:2])
                if k in (3, 4):
                    o = V.tensor_scalar(oh[k - 3][:, bass.ds(s, 1), :].rearrange("p a e -> p (a e)"), iota8[:, :],
                                        idxf[:, k - 3:k - 2], None, ALU.is_equal)
                if k == 5:
                    o = V.tensor_tensor(cnt[:, bass.ds(s, 1), :], oh[0][:, bass.ds(s, 1), :],
                                        oh[1][:, bass.ds(s, 1), :], ALU.add)
                o.then_inc(route, 1)

            def gates(i, k):
                dve.wait_ge(gap_act, i + 1)
                V.tensor_scalar(gate[k][:, bass.ds(i + 1, 1)], tgap[:, :], 0.5 - k, 0.5, ALU.mult, ALU.add)

            def accumulate(s, e, k):
                o = A[k][:, bass.ds(s, 1), :].rearrange("p a d -> p (a d)")
                w = oh[k][:, bass.ds(s, 1), e]
                if k == 0:
                    dve.wait_ge(down_ps, down_cnt(s, e))
                    dve.wait_ge(acc_done, down_cnt(s, e - 1))
                if e == 0:
                    r = V.tensor_scalar(o, ps_y, w, None, ALU.mult)
                else:
                    r = V.scalar_tensor_tensor(out=o, in0=ps_y, scalar=w, in1=o, op0=ALU.mult, op1=ALU.add)
                if k == 1:
                    r.then_inc(acc_done, 1)

            def side(i, t, half):
                if (t, half) == (1, 0):
                    yt_evac(i)
                if t % 4 == 2:
                    e = t // 4 - 2
                    accumulate(i + 1 if e >= 0 else i, e % E0, half)
                for k, at in enumerate(((3, 0), (3, 1), (4, 0), (4, 1), (5, 0), (5, 1))):
                    if at == (t, half):
                        route_step(i, k)
                if t == 9:
                    gates(i, half)

            with dve.Fori(0, BLOCKS) as i:
                for t in range(STEPS):
                    n = i * STEPS + t
                    Gp = G[:, :, (t - 1) % STEPS]
                    dve.wait_ge(r_act, n + 1)
                    dve.wait_ge(g_rdy, n + 1)
                    V.scalar_tensor_tensor(out=RH4[:, :], in0=tr[:, :], scalar=1.0, in1=Gp, op0=ALU.add, op1=ALU.mult).then_inc(rh_rdy, 1)
                    dve.wait_ge(z_act, n + 1)
                    V.scalar_tensor_tensor(out=Q4[:, :], in0=tz[:, :], scalar=1.0, in1=Gp, op0=ALU.add, op1=ALU.mult).then_inc(q_rdy, 1)
                    side(i, t, 0)
                    dve.wait_ge(h_act, n + 1)
                    V.scalar_tensor_tensor(out=P2[:, :], in0=tz[:, :], scalar=-1.0, in1=ht[:, :], op0=ALU.add, op1=ALU.mult).then_inc(p_rdy, 1)
                    dve.wait_ge(p_rdy, n + 2)
                    dve.wait_ge(q_rdy, n + 2)
                    if t == 0:
                        dve.wait_ge(yt_ps, i + 1)
                    V.scalar_tensor_tensor(out=G[:, :, t], in0=Q4[:, :], scalar=0.5, in1=P2[:, :], op0=ALU.mult, op1=ALU.subtract).then_inc(g_rdy, 1)
                    side(i, t, 1)

            yt_evac(BLOCKS)
            for k in range(2):
                accumulate(BLOCKS, 6, k)
            for k in range(N_ROUTE):
                route_step(BLOCKS, k)
            for k in range(2):
                gates(BLOCKS, k)
            for k in range(2):
                accumulate(BLOCKS, 7, k)
            for k in range(BLOCKS):
                if k == 0:
                    dve.wait_ge(route, N_ROUTE * SLOTS - N_ROUTE)
                else:
                    dve.wait_ge(pref_done, k)
                V.tensor_tensor(pref[:, k + 3, :], pref[:, k + 2, :], cnt[:, k + 2, :], ALU.add).then_inc(pref_done, 1)
            for e in range(3):
                for k in range(2):
                    accumulate(SLOTS - 1, e, k)
            dve.wait_ge(pos_ps, 1)
            V.tensor_scalar(kept[:, :, :], ps_misc[:, 0:BLOCKS * E0], float(CAP), None, ALU.is_lt).then_inc(keep_done, 1)
            for k in range(2):
                dve.wait_ge(keep_done, 3 * k + 1)
                V.tensor_tensor(kd[:, :, :], kept[:, :, :], oh[k][:, 2:, :], ALU.mult).then_inc(keep_done, 1)
                dve.wait_ge(keep_done, 3 * k + 2)
                V.tensor_reduce(kg[k][:, :], kd[:, :, :], AX_X, ALU.add).then_inc(keep_done, 1)
                dve.wait_ge(keep_done, 3 * k + 3)
                V.tensor_tensor(kg[k][:, :], kg[k][:, :], gate[k][:, 2:], ALU.mult).then_inc(keep_done, 1)
            dve.wait_ge(keep_done, 7)
            for e in range(3, E0):
                for k in range(2):
                    accumulate(SLOTS - 1, e, k)
            for k in range(BLOCKS):
                if k >= 2:
                    dve.wait_ge(x1_ps, k - 1)
                for j in range(2):
                    V.tensor_scalar(diag[j][:, k % 2, :], ident, kg[j][:, k:k + 1], None, ALU.mult).then_inc(diag_done, 1)
                if k >= 1:
                    dve.wait_ge(x1_ps, k)
                    V.tensor_tensor(x1p[:, :, KCONV - 1 + (k - 1) * STEPS:KCONV - 1 + k * STEPS],
                                    bank[(k - 1) % 2][:, 0:P].rearrange("p (b t) -> p b t", b=B),
                                    x_sb[:, (k - 1) * P:k * P].rearrange("p (b t) -> p b t", b=B), ALU.add).then_inc(x1_done, 1)
            k = BLOCKS
            dve.wait_ge(x1_ps, k)
            V.tensor_tensor(x1p[:, :, KCONV - 1 + (k - 1) * STEPS:KCONV - 1 + k * STEPS],
                            bank[(k - 1) % 2][:, 0:P].rearrange("p (b t) -> p b t", b=B),
                            x_sb[:, (k - 1) * P:k * P].rearrange("p (b t) -> p b t", b=B), ALU.add).then_inc(x1_done, 1)

            dve.wait_ge(in_rec, 16 * N_REC_IN)
            dve.wait_ge(x1_done, BLOCKS)
            V.tensor_scalar(conv[:, :, :], x1p[:, :, 0:T], h0[:, 0:1], cb[:, 0:1], ALU.mult, ALU.add).then_inc(rec, 1)
            for k in range(1, KCONV):
                dve.wait_ge(rec, k)
                o = V.scalar_tensor_tensor(out=conv[:, :, :], in0=x1p[:, :, k:k + T], scalar=h0[:, k:k + 1], in1=conv[:, :, :],
                                           op0=ALU.mult, op1=ALU.add)
                o.then_inc(rec if k < KCONV - 1 else conv_done, 1)
            for g in range(2):
                cols = slice(g * GRP, (g + 1) * GRP)
                dve.wait_ge(sp_act, 6 + 2 * g)
                V.tensor_tensor(Bg[:, cols], Bg[:, cols], Bt[:, cols], ALU.add).then_inc(rec, 1)
                dve.wait_ge(rec, 4 + 2 * g)
                dve.wait_ge(u_ps, g + 1)
                V.scalar_tensor_tensor(out=U[:, cols], in0=bank[g][0:NS, :], scalar=bs[:, 0:1], in1=Bg[:, cols],
                                       op0=ALU.add, op1=ALU.mult).then_inc(rec, 1)
            V.memset(sp_r[:, :], 0.0).then_inc(rec, 1)
            dve.wait_ge(rec, 8)
            for g in range(2):
                for b in (2 * g, 2 * g + 1):
                    V.tensor_tensor_scan(S[:, b * T:(b + 1) * T], decay_row[:, :], U[:, b * T:(b + 1) * T], 0.0,
                                         ALU.mult, ALU.add).then_inc(rec, 1)
                dve.wait_ge(c_act, 2)
                for b in (2 * g, 2 * g + 1):
                    dve.wait_ge(rec, 8 + 4 * g + 2)
                    cols = slice(b * T, (b + 1) * T)
                    V.scalar_tensor_tensor(out=Bg[:, cols], in0=S[:, cols], scalar=sp_v[:, 1:2], in1=Cg[:, cols],
                                           op0=ALU.mult, op1=ALU.mult).then_inc(rec, 1)

            dve.wait_ge(res_ps, 1)
            for h in range(2):
                V.tensor_copy(acc[:, h * MPG:(h + 1) * MPG, :], bank[6 + h][:, :]).then_inc(res_done, 1)

            def chained(o):
                rt_n[0] += 1
                o.then_inc(rt, 1)
                dve.wait_ge(rt, rt_n[0])

            rt_n = [0]
            dve.wait_ge(rl_ps, 1)
            chained(V.tensor_scalar(pr_e[:, :, :], bank[4][:, 0:TILES * 7].rearrange("p (m e) -> p m e", e=7),
                                    50.0, -50.0, ALU.min, ALU.max))
            dve.wait_ge(e_act, 1)
            chained(V.tensor_scalar(pr_e[:, :, :], pr_e[:, :, :], 1.0, None, ALU.add))
            chained(V.reciprocal(prob[:, :, 0:7], pr_e[:, :, :]))
            for m in range(TILES):
                o = V.max(out=ptop[:, m, :], in_=prob[:, m, :])
            chained(o)
            for m in range(TILES):
                o = V.max_index(out=pidx[:, m, :], in_max=ptop[:, m, :], in_values=prob[:, m, :])
            chained(o)
            V.tensor_copy(pidf[:, :], pidx[:, :, 0])
            chained(V.tensor_scalar(pw[:, :], ptop[:, :, 0], 1e-8, 1.0 - 1e-8, ALU.max, ALU.min))
            chained(V.tensor_scalar(ptw[:, :], pw[:, :], 0.5, 1e-8, ALU.add, ALU.add))
            chained(V.tensor_scalar(ptw[:, :], ptw[:, :], 0.5, 2.0, ALU.max, ALU.min))
            chained(V.reciprocal(prt[:, :], ptw[:, :]))
            chained(V.tensor_tensor(psel[:, :], pw[:, :], prt[:, :], ALU.mult))
            for m in range(TILES):
                o = V.tensor_scalar(wt[:, m, :], iota8[:, :], pidf[:, m:m + 1], psel[:, m:m + 1], ALU.is_equal, ALU.mult)
            chained(o)
            chained(V.tensor_scalar(wt[:, :, 7], prt[:, :], 0.5, None, ALU.mult))

            def gated(k):
                n = IC[k % 3]
                q = k // 3
                dve.wait_ge(g3_ps, k + 1)
                dve.wait_ge(silu_done, k + 1)
                if q >= 2:
                    dve.wait_ge(out_ps, q - 1)
                V.tensor_tensor(hh[0:n, q % 2, k % 3, :], sg[0:n, k % 2, :], bank[k % 2 * 2 + 1][0:n, :],
                                ALU.mult).then_inc(hh_done, 1)

            def add_expert(q):
                g, e = q // E1, q % E1
                dve.wait_ge(out_ps, q + 1)
                for m in range(MPG):
                    M = g * MPG + m
                    if e > 0:
                        dve.wait_ge(acc2, (q - 1) * MPG + m + 1)
                    V.scalar_tensor_tensor(out=acc[:, M, :], in0=bank[6 + q % 2][:, m * P:(m + 1) * P],
                                           scalar=wt[:, M, e:e + 1], in1=acc[:, M, :], op0=ALU.mult,
                                           op1=ALU.add).then_inc(acc2, 1)

            dve.wait_ge(res_done, 2)
            for q in range(2 * E1):
                for c in range(3):
                    gated(3 * q + c)
                if q >= 1:
                    add_expert(q - 1)
            add_expert(2 * E1 - 1)


def kernel(**inputs):
    import numpy as np
    import concourse.bacc as bacc
    from concourse.bass_utils import run_bass_kernel_spmd

    f = {k: np.asarray(v) for k, v in inputs.items()}
    c = lambda v: np.ascontiguousarray(v)
    L0, L1, M0, M1 = "L0_cond_", "L1_cond_", "L0_ffn_", "L1_ffn_"
    col = lambda v: v.reshape(-1, 1)
    tok = np.arange(P)
    b_of, t_of = tok // STEPS, tok % STEPS
    same = b_of[:, None] == b_of[None, :]
    before = same & (t_of[:, None] < t_of[None, :])
    below = b_of[:, None] < b_of[None, :]
    v1 = np.concatenate([f[M1 + "ew1"], f[M1 + "sw1"][None]])
    v3 = np.concatenate([f[M1 + "ew3"], f[M1 + "sw3"][None]])
    v2 = np.concatenate([f[M1 + "ew2"], f[M1 + "sw2"][None]])
    arrays = {
        "xT": c(f["x"].reshape(B, BLOCKS, STEPS, D).transpose(3, 1, 0, 2)).reshape(D, BLOCKS * P),
        "gw": c(np.stack([f[L0 + n].T for n in ("Wxr", "Wxz", "Wxh", "Whr", "Whz", "Whh", "Whq")], 1)),
        "gbias": c(np.stack([np.stack([f[L0 + "b" + s + g] for s in "xh"], 1) for g in "rzh"], 1)),
        "qbias": col(f[L0 + "bhq"]),
        "h0": c(f["cond_1024"].T),
        "consts": c(np.stack([np.eye(P), before, same, below], 1).astype(np.float32)),
        "iota8": np.broadcast_to(np.arange(8, dtype=np.float32), (P, 8)).copy(),
        "wg": f[M0 + "Wg"],
        "w1": c(f[M0 + "W1"].transpose(1, 0, 2)),
        "b1": c(f[M0 + "b1"].reshape(E0, HC, P).transpose(2, 0, 1)),
        "w2": c(f[M0 + "W2"].reshape(E0, HC, P, D).transpose(2, 0, 1, 3)),
        "b2": f[M0 + "b2"].reshape(1, E0, D),
        "wp": f[L1 + "Wp"], "ws": f[L1 + "Ws"], "wo": f[L1 + "Wo"],
        "cb": col(f[L1 + "conv_b"]), "bpb": c(f[L1 + "bp"].reshape(2, NS).T), "bs": col(f[L1 + "bs"]), "bo": col(f[L1 + "bo"]),
        "alog": c(np.stack([f[L1 + "A_log"], f[L1 + "dt_log"]], 1)),
        "rw": c(f[M1 + "router_w"].T), "rb": f[M1 + "routing_bias"].reshape(1, 7),
        "v1": c(v1.transpose(2, 0, 1)), "v3": c(v3.transpose(2, 0, 1)),
        "v2a": c(v2[:, :, :2 * P].reshape(E1, D, 2, P).transpose(3, 0, 2, 1)),
        "v2b": c(v2[:, :, 2 * P:].transpose(2, 0, 1)),
    }
    nc = bacc.Bacc("TRN2", target_bir_lowering=False, num_devices=1)
    args = {k: nc.dram_tensor("in_" + k, v.shape, F32, kind="ExternalInput").ap() for k, v in arrays.items()}
    out = nc.dram_tensor("out", (B * T, D), F32, kind="ExternalOutput").ap()
    adaln_ffn_kernel(nc, args, out)
    r = run_bass_kernel_spmd(nc, [{"in_" + k: v for k, v in arrays.items()}], core_ids=[0])
    return np.asarray(r.results[0]["out"]).reshape(B, T, D)
```

```python
from contextlib import ExitStack

import concourse.bass as bass
from concourse import mybir

F32 = mybir.dt.float32
BF16 = mybir.dt.bfloat16
U32 = mybir.dt.uint32
ALU = mybir.AluOpType
ACT = mybir.ActivationFunctionType
AX_X = mybir.AxisListType.X

P = 128
B, T, D = 4, 256, 128
STEPS = 32
BLOCKS = T // STEPS
SLOTS = BLOCKS + 1
E0, H0 = 8, 512
HC = H0 // P
CAP = 269
NS = 64
KCONV = 4
E1, I1 = 8, 352
WARM_A, WARM_B = 480, 480
WARM_FIRST = 512
IC = (128, 128, 96)
TILES = B * T // P
GRP = 512
MPG = GRP // P


def adaln_ffn_kernel(nc, a, out):
    with ExitStack() as ctx:
        def sb(name, shape, dt=F32):
            return ctx.enter_context(nc.sbuf_tensor(name, shape, dt))

        def psum(name):
            return ctx.enter_context(nc.psum_tensor(name, [P, 512], F32))

        def sem(name):
            return ctx.enter_context(nc.semaphore(name))

        x_sb = sb("x_sb", [P, BLOCKS * P])
        gw = sb("gw", [P, 7, P])
        gbias = sb("gbias", [P, 3, 2])
        qbias = sb("qbias", [P, 1])
        h0 = sb("h0", [P, B])
        consts = sb("consts", [P, 4, P])
        iota8 = sb("iota8", [P, 8])
        wg = sb("wg", [P, E0])
        w1 = sb("w1", [P, E0, H0])
        b1 = sb("b1", [P, E0, HC])
        w2 = sb("w2", [P, E0, HC, D])
        b2 = sb("b2", [BLOCKS * E0, BLOCKS, D])
        ident, m_before, m_same, m_below = (consts[:, k, :] for k in range(4))

        gws = sb("gws", [P, 5, P])
        wr_q, wr_p, wz_g, wh_rh, wq_g = (gws[:, k, :] for k in range(5))
        gb = sb("gb", [P, 3])
        xp = sb("xp", [P, 3, (BLOCKS + 1) * P])
        G = sb("G", [P, B, STEPS])
        Q4 = sb("Q4", [P, B])
        P2 = sb("P2", [P, B])
        RH4 = sb("RH4", [P, B])
        tr = sb("tr", [P, B])
        tz = sb("tz", [P, B])
        ht = sb("ht", [P, B])
        yT = sb("yT", [P, P])
        hT = [sb("hT%d" % k, [P, HC, P]) for k in range(2)]
        ones_row = sb("ones_row", [1, P])
        warm = sb("warm", [P, 512], BF16)
        lg = sb("lg", [P, E0])
        top8 = sb("top8", [P, 8])
        idx8 = sb("idx8", [P, 8], U32)
        idxf = sb("idxf", [P, 2])
        gap = sb("gap", [P, 1])
        tgap = sb("tgap", [P, 1])
        gate = [sb("gate%d" % k, [P, SLOTS]) for k in range(2)]
        oh = [sb("oh%d" % k, [P, SLOTS, E0]) for k in range(2)]
        cnt = sb("cnt", [P, SLOTS, E0])
        A = [sb("A%d" % k, [P, SLOTS, D]) for k in range(2)]

        pref = sb("pref", [P, SLOTS + 1, E0])
        kept = sb("kept", [P, BLOCKS, E0])
        kd = [sb("kd%d" % k, [P, BLOCKS, E0]) for k in range(2)]
        ck = sb("ck", [P, BLOCKS, E0])
        ckT = sb("ckT", [BLOCKS * E0, P])
        kg = [sb("kg%d" % k, [P, BLOCKS]) for k in range(2)]
        diag = [sb("diag%d" % k, [P, 2, P]) for k in range(2)]
        x1p = sb("x1p", [P, B, KCONV - 1 + T])

        wp = sb("wp", [P, 2 * NS])
        ws = sb("ws", [P, NS])
        wo = sb("wo", [P, D])
        cb = sb("cb", [P, 1])
        bpb = sb("bpb", [P, 2])
        bs = sb("bs", [P, 1])
        bo = sb("bo", [P, 1])
        alog = sb("alog", [P, 2])
        sp_t = sb("sp_t", [P, 2])
        sp_r = sb("sp_r", [P, 2])
        sp_v = sb("sp_v", [P, 2])
        decay = sb("decay", [P, 1])
        decay_row = sb("decay_row", [P, T])
        conv = sb("conv", [P, B, T])
        Cg = sb("Cg", [P, GRP])
        Bg = sb("Bg", [P, GRP])
        Bt = sb("Bt", [P, GRP])
        U = sb("U", [P, GRP])
        S = sb("S", [P, GRP])
        Yg = sb("Yg", [P, GRP])
        xc = sb("xc", [P, B * T])

        rw = sb("rw", [P, 7])
        rb = sb("rb", [1, 7])
        v1 = sb("v1", [P, E1, I1])
        v3 = sb("v3", [P, E1, I1])
        v2a = sb("v2a", [P, E1, 2, D])
        v2b = sb("v2b", [IC[2], E1, D])
        prob = sb("prob", [P, TILES, 8])
        pr_e = sb("pr_e", [P, TILES, 7])
        ptop = sb("ptop", [P, TILES, 8])
        pidx = sb("pidx", [P, TILES, 8], U32)
        pidf = sb("pidf", [P, TILES])
        pw = sb("pw", [P, TILES])
        ptw = sb("ptw", [P, TILES])
        prt = sb("prt", [P, TILES])
        psel = sb("psel", [P, TILES])
        wt = sb("wt", [P, TILES, 8])
        sg = sb("sg", [P, 2, GRP])
        hh = sb("hh", [P, 2, 3, GRP])
        acc = sb("acc", [P, TILES, D])

        bank = [psum("bank%d" % k) for k in range(8)]
        pre = [bank[g][:, 0:P].rearrange("p (b t) -> p b t", b=B) for g in range(3)]
        ps_h = [bank[3 + k][:, :].rearrange("p (c t) -> p c t", c=HC) for k in range(2)]
        ps_y = bank[5][:, 0:D]
        ps_misc = bank[6]
        ps_warm = bank[7][:, :]

        in_gru, in_moe, in_rec, in_l1 = sem("in_gru"), sem("in_moe"), sem("in_rec"), sem("in_l1")
        pool_set = sem("pool_set")
        weights_scaled, gbias_sum = sem("weights_scaled"), sem("gbias_sum")
        xp_ps, xp_done, xp_used = sem("xp_ps"), sem("xp_done"), sem("xp_used")
        r_pre, z_pre, h_pre = sem("r_pre"), sem("z_pre"), sem("h_pre")
        r_act, z_act, h_act = sem("r_act"), sem("z_act"), sem("h_act")
        rh_rdy, q_rdy, p_rdy, g_rdy = sem("rh_rdy"), sem("q_rdy"), sem("p_rdy"), sem("g_rdy")
        yt_ps, yt_done, lg_ps, route, gap_act = sem("yt_ps"), sem("yt_done"), sem("lg_ps"), sem("route"), sem("gap_act")
        up_ps, gelu_done, down_ps, acc_done = sem("up_ps"), sem("gelu_done"), sem("down_ps"), sem("acc_done")
        pref_done, pos_ps, keep_done = sem("pref_done"), sem("pos_ps"), sem("keep_done")
        diag_done, x1_ps, x1_done = sem("diag_done"), sem("x1_ps"), sem("x1_done")
        ckt_ps, ckt_done, conv_step, keep_last = sem("ckt_ps"), sem("ckt_done"), sem("conv_step"), sem("keep_last")
        dec_act, dec_dve = sem("dec_act"), sem("dec_dve")
        conv_done, cproj_ps, bproj_ps, u_ps = sem("conv_done"), sem("cproj_ps"), sem("bproj_ps"), sem("u_ps")
        sp_act, c_act, rec = sem("sp_act"), sem("c_act"), sem("rec")
        xc_ps, xc_done = sem("xc_ps"), sem("xc_done")
        rl_ps, rt, e_act = sem("rl_ps"), sem("rt"), sem("e_act")
        res_ps, res_done = sem("res_ps"), sem("res_done")
        g1_ps, g3_ps, silu_done, hh_done, out_ps, acc2 = (sem("g1_ps"), sem("g3_ps"), sem("silu_done"),
                                                         sem("hh_done"), sem("out_ps"), sem("acc2"))
        stored = sem("stored")

        def up_cnt(s, e):
            return 8 * (s - 1) + e + 2

        def gelu_cnt(s, e):
            return 8 * (s - 1) + e + 3

        def down_cnt(s, e):
            return 8 * (s - 1) + e + 4

        N_ROUTE = 6
        N_GRU_IN, N_MOE_IN, N_REC_IN, N_L1_IN = 7, 6, 8, 5

        block = ctx.enter_context(nc.Block())

        @block.sync
        def _(sp):
            for dst, src in ((x_sb[:, 0:BLOCKS * P], "xT"), (gw[:, :, :], "gw"), (gbias[:, :, :], "gbias"),
                             (qbias[:, :], "qbias"), (h0[:, :], "h0"), (consts[:, :, :], "consts"),
                             (alog[:, :], "alog")):
                sp.dma_start(dst, a[src]).then_inc(in_gru, 16)
            for dst, src in ((wg[:, :], "wg"), (w1[:, :, :], "w1"), (b1[:, :, :], "b1"), (w2[:, :, :, :], "w2"),
                             (b2[:, :, :], "b2"), (iota8[:, :], "iota8")):
                sp.dma_start(dst, a[src]).then_inc(in_moe, 16)
            for dst, src in ((wp[:, :], "wp"), (ws[:, :], "ws"), (wo[:, :], "wo"), (cb[:, :], "cb"),
                             (bpb[:, :], "bpb"), (bs[:, :], "bs"), (bo[:, :], "bo"), (rw[:, :], "rw")):
                sp.dma_start(dst, a[src]).then_inc(in_rec, 16)
            for dst, src in ((rb[:, :], "rb"), (v1[:, :, :], "v1"), (v3[:, :, :], "v3"),
                             (v2a[:, :, :, :], "v2a"), (v2b[:, :, :], "v2b")):
                sp.dma_start(dst, a[src]).then_inc(in_l1, 16)
            for g in range(2):
                sp.wait_ge(acc2, E1 * MPG * (g + 1))
                sp.dma_start(out[g * GRP:(g + 1) * GRP, :].rearrange("(m p) d -> p m d", p=P),
                             acc[:, g * MPG:(g + 1) * MPG, :]).then_inc(stored, 16)
            sp.wait_ge(stored, 32)

        @block.gpsimd
        def _(pool):
            nc.gpsimd.memset(xp[:, :, BLOCKS * P:], 0.0)
            nc.gpsimd.memset(ones_row[:, :], 1.0)
            nc.gpsimd.memset(warm[:, :], 1.0)
            nc.gpsimd.memset(x1p[:, :, 0:KCONV - 1], 0.0)
            nc.gpsimd.memset(hT[0][:, :, :], 0.0)
            nc.gpsimd.memset(hT[1][:, :, :], 0.0).then_inc(gelu_done, 1)
            nc.gpsimd.memset(oh[0][:, 0, :], 0.0)
            nc.gpsimd.memset(oh[1][:, 0, :], 0.0)
            nc.gpsimd.memset(A[0][:, 0, :], 0.0)
            nc.gpsimd.memset(A[1][:, 0, :], 0.0).then_inc(down_ps, 1)
            nc.gpsimd.memset(prob[:, :, :], -1.0)
            nc.gpsimd.memset(pref[:, 0:2, :], 0.0).then_inc(pool_set, 1)

        @block.tensor
        def _(pe):
            def mm(o, lhsT, rhs, start=False, stop=False):
                return nc.tensor.matmul(o, lhsT, rhs, start=start, stop=stop, skip_group_check=True)

            def keep_warm(n):
                mm(ps_warm[:, 0:n], warm[:, 0:P], warm[:, 0:n], start=True, stop=True)

            def x_products(i):
                if i >= 1:
                    pe.wait_ge(xp_done, i)
                for g in range(3):
                    last = mm(ps_misc[:, g * P:(g + 1) * P], gw[:, g, :], x_sb[:, i * P:(i + 1) * P],
                              start=(g == 0), stop=True)
                last.then_inc(xp_ps, 1)

            def inject(g, i):
                return mm(bank[g][:, 0:P], ident, xp[:, g, bass.ds(i * P, P)], start=True)

            def y_product(i):
                pe.wait_ge(g_rdy, i * STEPS + 1)
                mm(ps_misc[:, 0:P], wq_g, G[:, :, :].rearrange("p b t -> p (b t)"), start=True, stop=True)\
                    .then_inc(yt_ps, 1)

            def router_product(s):
                pe.wait_ge(yt_done, s)
                mm(ps_misc[:, 0:E0], yT[:, :], wg[:, :], start=True, stop=True).then_inc(lg_ps, 1)

            def up(s, e, c):
                if c == 0:
                    pe.wait_ge(gelu_done, gelu_cnt(s, e - 2))
                    if e == 0:
                        pe.wait_ge(yt_done, s)
                m = mm(ps_h[e % 2][:, c, :], w1[:, e, c * P:(c + 1) * P], yT[:, :], start=(c == 0), stop=True)
                if c == HC - 1:
                    m.then_inc(up_ps, 1)

            def down(s, e, c):
                if c == 0:
                    pe.wait_ge(gelu_done, gelu_cnt(s, e))
                    pe.wait_ge(acc_done, down_cnt(s, e - 1))
                m = mm(ps_y, hT[e % 2][:, c, :], w2[:, e, c, :], start=(c == 0), stop=(c == HC - 1))
                if c == HC - 1:
                    m.then_inc(down_ps, 1)

            def side(i, t, half):
                if t % 4 in (2, 3):
                    up(i, t // 4, (t % 4 - 2) * 2 + half)
                else:
                    e = t // 4 - 2
                    down(i if e >= 0 else i - 1, e % E0, (t % 4) * 2 + half)
                if (t, half) == (0, 1):
                    y_product(i)
                if (t, half) == (1, 1):
                    router_product(i)

            def first_side(i, t, half):
                keep_warm(WARM_FIRST)
                if half == 1 and t % 4 == 1 and t // 4 + 1 < BLOCKS:
                    x_products(t // 4 + 1)

            def gru_block(i, side):
                for t in range(STEPS):
                    n = i * STEPS + t
                    pe.wait_ge(q_rdy, n + 1)
                    mm(pre[0][:, :, t], wr_q, Q4[:, :])
                    pe.wait_ge(p_rdy, n + 1)
                    mm(pre[0][:, :, t], wr_p, P2[:, :]).then_inc(r_pre, 1)
                    if t == 0:
                        inject(1, i)
                    else:
                        side(i, t, 0)
                    pe.wait_ge(g_rdy, n + 1)
                    mm(pre[1][:, :, t], wz_g, G[:, :, (t - 1) % STEPS]).then_inc(z_pre, 1)
                    if t == 0:
                        inject(2, i)
                    keep_warm(WARM_A)
                    pe.wait_ge(rh_rdy, n + 1)
                    mm(pre[2][:, :, t], wh_rh, RH4[:, :], stop=True).then_inc(h_pre, 1)
                    if t == 0:
                        side(i, 0, 0)
                    side(i, t, 1)
                    keep_warm(WARM_B)
                inject(0, i + 1)

            pe.wait_ge(in_gru, 16 * N_GRU_IN)
            pe.wait_ge(pool_set, 1)
            x_products(0)
            for _ in range(16):
                keep_warm(512)
            pe.wait_ge(xp_done, 1)
            inject(0, 0)
            pe.wait_ge(weights_scaled, 5)
            gru_block(0, first_side)
            pe.wait_ge(in_moe, 16 * N_MOE_IN)
            with pe.Fori(1, BLOCKS) as i:
                gru_block(i, side)

            last_slot = SLOTS - 1
            y_product(BLOCKS)
            for c in range(HC):
                down(last_slot - 1, 6, c)
            router_product(last_slot)
            for c in range(HC):
                down(last_slot - 1, 7, c)

            def positions():
                pe.wait_ge(pref_done, BLOCKS)
                o = ps_misc[:, 0:BLOCKS * E0]
                mm(o, m_before, cnt[:, 1:, :], start=True)
                mm(o, m_same, pref[:, 1:SLOTS, :])
                mm(o, m_below, pref[:, SLOTS:SLOTS + 1, :].to_broadcast([P, BLOCKS, E0]), stop=True).then_inc(pos_ps, 1)

            def x1_product(k):
                pe.wait_ge(diag_done, 2 * k + 2)
                if k >= 2:
                    pe.wait_ge(x1_done, k - 1)
                if k == BLOCKS - 1:
                    pe.wait_ge(acc_done, down_cnt(last_slot, E0 - 1))
                o = bank[k % 2][:, 0:P]
                mm(o, A[0][:, k + 1, :], diag[0][:, k % 2, :], start=True)
                mm(o, A[1][:, k + 1, :], diag[1][:, k % 2, :])
                mm(o, b2[:, k, :], ckT[:, :], stop=True).then_inc(x1_ps, 1)

            for e in range(E0 + 2):
                if e < E0:
                    for c in range(HC):
                        up(last_slot, e, c)
                if e == 0:
                    positions()
                if e >= 2:
                    for c in range(HC):
                        down(last_slot, e - 2, c)
                if e == 2:
                    pe.wait_ge(keep_last, 1)
                    mm(bank[7][0:BLOCKS * E0, 0:P], ck[:, :, :].rearrange("p k e -> p (k e)"), ident, start=True, stop=True)\
                        .then_inc(ckt_ps, 1)
                if e == 3:
                    pe.wait_ge(ckt_done, 1)
                if 3 <= e:
                    x1_product(e - 3)
            x1_product(BLOCKS - 1)

            pe.wait_ge(in_rec, 16 * N_REC_IN)
            pe.wait_ge(conv_step, 8)

            def project(o, w, source):
                for g in range(2):
                    last = mm(o[NS * g:NS * (g + 1), :], w, source(g), start=True, stop=True)
                return last

            project(bank[2], wp[:, NS:], lambda g: conv[:, 2 * g:2 * g + 2, :]).then_inc(cproj_ps, 1)
            project(bank[3], wp[:, 0:NS], lambda g: conv[:, 2 * g:2 * g + 2, :]).then_inc(bproj_ps, 1)
            project(bank[4], ws[:, :], lambda g: x1p[:, 2 * g:2 * g + 2, KCONV - 1:]).then_inc(u_ps, 1)
            pe.wait_ge(in_l1, 16 * N_L1_IN)
            for m in range(TILES):
                b, h = m // 2, m % 2
                last = mm(bank[6 + m // 4][:, (m % 4) * P:(m % 4 + 1) * P],
                          x1p[:, b, KCONV - 1 + h * P:KCONV - 1 + (h + 1) * P], ident, start=(m % 4 == 0), stop=True)
            last.then_inc(res_ps, 1)
            for g in range(2):
                if g == 0:
                    pe.wait_ge(rec, 6)
                rows = slice(NS * g, NS * (g + 1))
                mm(bank[g][:, :], wo[rows, :], Yg[rows, :], start=True, stop=True).then_inc(xc_ps, 1)
            pe.wait_ge(xc_done, 2)
            for m in range(TILES):
                o = bank[4][:, m * 7:(m + 1) * 7]
                mm(o, xc[:, m * P:(m + 1) * P], rw[:, :], start=(m == 0))
                last = mm(o, ones_row[:, :], rb[:, :], stop=True)
            last.then_inc(rl_ps, 1)

            def ups(g, e, c):
                k = (g * E1 + e) * 3 + c
                n = IC[c]
                cols = slice(c * P, c * P + n)
                rhs = xc[:, g * GRP:(g + 1) * GRP]
                if k >= 2:
                    pe.wait_ge(hh_done, k - 1)
                if k < 1:
                    pe.wait_ge(xc_done, 2)
                mm(bank[k % 2 * 2][0:n, :], v1[:, e, cols], rhs, start=True, stop=True).then_inc(g1_ps, 1)
                mm(bank[k % 2 * 2 + 1][0:n, :], v3[:, e, cols], rhs, start=True, stop=True).then_inc(g3_ps, 1)

            def outs(g, e):
                q = g * E1 + e
                pe.wait_ge(hh_done, 3 * q + 3)
                if q < 2:
                    pe.wait_ge(res_done, 2)
                else:
                    pe.wait_ge(acc2, MPG * (q - 1))
                for m in range(MPG):
                    o = bank[6 + q % 2][:, m * P:(m + 1) * P]
                    for c in range(3):
                        w = v2a[:, e, c, :] if c < 2 else v2b[:, e, :]
                        last = mm(o, hh[0:IC[c], q % 2, c, m * P:(m + 1) * P], w,
                                  start=(m == 0 and c == 0), stop=(c == 2))
                last.then_inc(out_ps, 1)

            for q in range(2 * E1 + 1):
                if q < 2 * E1:
                    for c in range(3):
                        ups(q // E1, q % E1, c)
                if q >= 1:
                    outs((q - 1) // E1, (q - 1) % E1)

        @block.scalar
        def _(act):
            nc.scalar.preload_act_table_set("natural_log_exp_and_others")
            act.wait_ge(in_gru, 16 * N_GRU_IN)
            nc.scalar.activation(sp_t[:, :], alog[:, :], ACT.Abs).then_inc(dec_act, 1)
            act.wait_ge(dec_act, 1)
            nc.scalar.activation(sp_t[:, :], sp_t[:, :], ACT.Exp, scale=-1.0).then_inc(dec_act, 1)
            act.wait_ge(dec_act, 2)
            nc.scalar.activation(sp_t[:, :], sp_t[:, :], ACT.Ln, bias=1.0).then_inc(dec_act, 1)
            nc.scalar.activation(sp_r[:, :], alog[:, :], ACT.Relu).then_inc(dec_act, 1)
            nc.scalar.preload_act_table_set("gelu_apprx_tanh_and_others")

            def xp_evac(g, k):
                o = nc.scalar.activation(xp[:, g, k * P:(k + 1) * P], ps_misc[:, g * P:(g + 1) * P], ACT.Identity,
                                         bias=gb[:, g:g + 1])
                if g == 2:
                    o.then_inc(xp_done, 1)

            def gelu(s, e, c):
                if c == 0:
                    act.wait_ge(up_ps, up_cnt(s, e))
                    act.wait_ge(down_ps, down_cnt(s, e - 2))
                g = nc.scalar.activation(hT[e % 2][:, c, :], ps_h[e % 2][:, c, :], ACT.Gelu_apprx_tanh,
                                         bias=b1[:, e, c:c + 1])
                if c == HC - 1:
                    g.then_inc(gelu_done, 1)

            def gap_tanh(s):
                act.wait_ge(route, N_ROUTE * (s - 1) + 2)
                nc.scalar.activation(tgap[:, :], gap[:, :], ACT.Tanh, scale=0.5).then_inc(gap_act, 1)

            act.wait_ge(gbias_sum, 1)
            act.wait_ge(xp_ps, 1)
            for g in range(3):
                xp_evac(g, 0)

            def side(i, t):
                e = t // 4 - 1
                gelu(i if e >= 0 else i - 1, e % E0, t % 4)

            def late_side(i, t):
                if t == 8:
                    gap_tanh(i)

            def first_side(i, t):
                k = t // 4 + 1
                if t % 4 == 3 and k < BLOCKS:
                    act.wait_ge(xp_ps, k + 1)
                    for g in range(3):
                        xp_evac(g, k)

            def gru_block(i, side, late_side):
                for t in range(STEPS):
                    n = i * STEPS + t
                    act.wait_ge(r_pre, n + 1)
                    nc.scalar.activation(tr[:, :], pre[0][:, :, t], ACT.Tanh, scale=0.5).then_inc(r_act, 1)
                    side(i, t)
                    act.wait_ge(z_pre, n + 1)
                    nc.scalar.activation(tz[:, :], pre[1][:, :, t], ACT.Tanh, scale=0.5).then_inc(z_act, 1)
                    act.wait_ge(h_pre, n + 1)
                    nc.scalar.activation(ht[:, :], pre[2][:, :, t], ACT.Tanh).then_inc(h_act, 1)
                    late_side(i, t)

            gru_block(0, first_side, lambda i, t: None)
            act.wait_ge(in_moe, 16 * N_MOE_IN)
            act.wait_ge(pool_set, 1)
            with act.Fori(1, BLOCKS) as i:
                gru_block(i, side, late_side)
            for c in range(HC):
                gelu(SLOTS - 2, 7, c)
            for e in range(E0):
                for c in range(HC):
                    gelu(SLOTS - 1, e, c)
                if e == 0:
                    gap_tanh(SLOTS - 1)

            act.wait_ge(in_rec, 16 * N_REC_IN)
            act.wait_ge(cproj_ps, 1)
            nc.scalar.activation(Cg[:, :], bank[2][:, :], ACT.Tanh, bias=bpb[:, 1:2]).then_inc(c_act, 1)
            nc.scalar.preload_act_table_set("natural_log_exp_and_others")
            act.wait_ge(bproj_ps, 1)
            nc.scalar.activation(Bt[:, :], bank[3][:, :], ACT.Abs, bias=bpb[:, 0:1]).then_inc(sp_act, 1)
            nc.scalar.activation(Bg[:, :], bank[3][:, :], ACT.Relu, bias=bpb[:, 0:1]).then_inc(sp_act, 1)
            act.wait_ge(sp_act, 1)
            nc.scalar.activation(Bt[:, :], Bt[:, :], ACT.Exp, scale=-1.0).then_inc(sp_act, 1)
            act.wait_ge(sp_act, 3)
            nc.scalar.activation(Bt[:, :], Bt[:, :], ACT.Ln, bias=1.0).then_inc(sp_act, 1)
            for g in range(2):
                act.wait_ge(xc_ps, g + 1)
                nc.scalar.activation(xc[:, g * GRP:(g + 1) * GRP], bank[g][:, :], ACT.Identity,
                                     bias=bo[:, 0:1]).then_inc(xc_done, 1)
            act.wait_ge(rt, 1)
            nc.scalar.activation(pr_e[:, :, :], pr_e[:, :, :], ACT.Exp, scale=-1.0).then_inc(e_act, 1)
            nc.scalar.preload_act_table_set("silu_and_others")
            for k in range(2 * E1 * 3):
                n = IC[k % 3]
                act.wait_ge(g1_ps, k + 1)
                if k >= 2:
                    act.wait_ge(hh_done, k - 1)
                nc.scalar.activation(sg[0:n, k % 2, :], bank[k % 2 * 2][0:n, :], ACT.Silu).then_inc(silu_done, 1)

        @block.vector
        def _(dve):
            V = nc.vector
            dve.wait_ge(in_gru, 16 * N_GRU_IN)
            V.tensor_tensor(gb[:, :], gbias[:, :, 0], gbias[:, :, 1], ALU.add).then_inc(gbias_sum, 1)
            for k, (src, f) in enumerate(((3, 0.25), (3, -0.5), (4, 0.5), (5, 0.25), (6, 0.5))):
                V.tensor_scalar(gws[:, k, :], gw[:, src, :], f, None, ALU.mult).then_inc(weights_scaled, 1)
            V.memset(bank[4][:, :], 0.0).then_inc(up_ps, 1)
            dve.wait_ge(pool_set, 1)
            V.tensor_scalar(Q4[:, :], h0[:, :], 4.0, None, ALU.mult).then_inc(q_rdy, 1)
            V.memset(P2[:, :], 0.0).then_inc(p_rdy, 1)
            V.memset(G[:, :, :], 0.0).then_inc(acc_done, 1)
            dve.wait_ge(acc_done, 1)
            V.tensor_scalar(G[:, :, STEPS - 1], h0[:, :], 2.0, None, ALU.mult).then_inc(g_rdy, 1)
            dve.wait_ge(dec_act, 4)
            V.tensor_tensor(sp_v[:, :], sp_t[:, :], sp_r[:, :], ALU.add).then_inc(dec_dve, 1)
            dve.wait_ge(dec_dve, 1)
            V.tensor_tensor(decay[:, :], sp_v[:, 0:1], sp_v[:, 1:2], ALU.mult).then_inc(dec_dve, 1)
            dve.wait_ge(dec_dve, 2)
            V.tensor_scalar(decay[:, :], decay[:, :], -1.0, 1.0, ALU.mult, ALU.add).then_inc(dec_dve, 1)
            dve.wait_ge(dec_dve, 3)
            V.tensor_copy(decay_row[:, :], decay[:, 0:1].to_broadcast([P, T])).then_inc(dec_dve, 1)

            def yt_evac(s):
                dve.wait_ge(yt_ps, s)
                dve.wait_ge(up_ps, up_cnt(s - 1, E0 - 1))
                V.tensor_scalar(yT[:, :], ps_misc[:, 0:P], qbias[:, 0:1], None, ALU.add).then_inc(yt_done, 1)

            def route_step(s, k):
                if k == 0:
                    dve.wait_ge(lg_ps, s)
                    V.tensor_copy(lg[:, :], ps_misc[:, 0:E0])
                    o = V.max(out=top8[:, :], in_=ps_misc[:, 0:E0])
                else:
                    dve.wait_ge(route, N_ROUTE * (s - 1) + k)
                if k == 1:
                    V.tensor_tensor(gap[:, :], top8[:, 0:1], top8[:, 1:2], ALU.subtract)
                    o = V.max_index(out=idx8[:, :], in_max=top8[:, :], in_values=lg[:, :])
                if k == 2:
                    o = V.tensor_copy(idxf[:, :], idx8[:, 0:2])
                if k in (3, 4):
                    o = V.tensor_scalar(oh[k - 3][:, bass.ds(s, 1), :].rearrange("p a e -> p (a e)"), iota8[:, :],
                                        idxf[:, k - 3:k - 2], None, ALU.is_equal)
                if k == 5:
                    o = V.tensor_tensor(cnt[:, bass.ds(s, 1), :], oh[0][:, bass.ds(s, 1), :],
                                        oh[1][:, bass.ds(s, 1), :], ALU.add)
                o.then_inc(route, 1)

            def gates(s, k):
                dve.wait_ge(gap_act, s)
                V.tensor_scalar(gate[k][:, bass.ds(s, 1)], tgap[:, :], 0.5 - k, 0.5, ALU.mult, ALU.add)

            def accumulate(s, e, k):
                o = A[k][:, bass.ds(s, 1), :].rearrange("p a d -> p (a d)")
                w = oh[k][:, bass.ds(s, 1), e]
                if k == 0:
                    dve.wait_ge(down_ps, down_cnt(s, e))
                    dve.wait_ge(acc_done, down_cnt(s, e - 1))
                if e == 0:
                    r = V.tensor_scalar(o, ps_y, w, None, ALU.mult)
                else:
                    r = V.scalar_tensor_tensor(out=o, in0=ps_y, scalar=w, in1=o, op0=ALU.mult, op1=ALU.add)
                if k == 1:
                    r.then_inc(acc_done, 1)

            def side(i, t, half):
                if (t, half) == (1, 0):
                    yt_evac(i)
                if t % 4 == 2:
                    e = t // 4 - 2
                    accumulate(i if e >= 0 else i - 1, e % E0, half)
                for k, at in enumerate(((3, 0), (3, 1), (4, 0), (4, 1), (5, 0), (5, 1))):
                    if at == (t, half):
                        route_step(i, k)
                if t == 9:
                    gates(i, half)

            def gru_block(i, side):
                for t in range(STEPS):
                    n = i * STEPS + t
                    Gp = G[:, :, (t - 1) % STEPS]
                    dve.wait_ge(r_act, n + 1)
                    dve.wait_ge(g_rdy, n + 1)
                    V.scalar_tensor_tensor(out=RH4[:, :], in0=tr[:, :], scalar=1.0, in1=Gp, op0=ALU.add, op1=ALU.mult).then_inc(rh_rdy, 1)
                    dve.wait_ge(z_act, n + 1)
                    V.scalar_tensor_tensor(out=Q4[:, :], in0=tz[:, :], scalar=1.0, in1=Gp, op0=ALU.add, op1=ALU.mult).then_inc(q_rdy, 1)
                    side(i, t, 0)
                    dve.wait_ge(h_act, n + 1)
                    V.scalar_tensor_tensor(out=P2[:, :], in0=tz[:, :], scalar=-1.0, in1=ht[:, :], op0=ALU.add, op1=ALU.mult).then_inc(p_rdy, 1)
                    dve.wait_ge(p_rdy, n + 2)
                    dve.wait_ge(q_rdy, n + 2)
                    if t == 0 and side is not no_side:
                        dve.wait_ge(yt_ps, i)
                    V.scalar_tensor_tensor(out=G[:, :, t], in0=Q4[:, :], scalar=0.5, in1=P2[:, :], op0=ALU.mult, op1=ALU.subtract).then_inc(g_rdy, 1)
                    side(i, t, 1)

            def no_side(i, t, half):
                pass

            gru_block(0, no_side)
            dve.wait_ge(in_moe, 16 * N_MOE_IN)
            with dve.Fori(1, BLOCKS) as i:
                gru_block(i, side)

            last = SLOTS - 1
            yt_evac(last)
            for k in range(BLOCKS - 1):
                if k >= 1:
                    dve.wait_ge(pref_done, k)
                V.tensor_tensor(pref[:, k + 2, :], pref[:, k + 1, :], cnt[:, k + 1, :], ALU.add).then_inc(pref_done, 1)
            for k in range(2):
                accumulate(last - 1, 6, k)
            for k in range(N_ROUTE):
                route_step(last, k)
            dve.wait_ge(route, N_ROUTE * last)
            dve.wait_ge(pref_done, BLOCKS - 1)
            V.tensor_tensor(pref[:, SLOTS, :], pref[:, SLOTS - 1, :], cnt[:, SLOTS - 1, :], ALU.add).then_inc(pref_done, 1)
            for k in range(2):
                accumulate(last - 1, 7, k)
            for k in range(2):
                gates(last, k)
            dve.wait_ge(pos_ps, 1)
            V.tensor_scalar(kept[:, :, :], ps_misc[:, 0:BLOCKS * E0].rearrange("p (k e) -> p k e", e=E0), float(CAP), None,
                            ALU.is_lt).then_inc(keep_done, 1)
            dve.wait_ge(keep_done, 1)
            for k in range(2):
                V.tensor_tensor(kd[k][:, :, :], kept[:, :, :], oh[k][:, 1:, :], ALU.mult).then_inc(keep_done, 1)
            for k in range(2):
                dve.wait_ge(keep_done, 2 + k)
                V.tensor_reduce(kg[k][:, :], kd[k][:, :, :], AX_X, ALU.add).then_inc(keep_done, 1)
            for k in range(2):
                dve.wait_ge(keep_done, 4 + k)
                V.tensor_tensor(kg[k][:, :], kg[k][:, :], gate[k][:, 1:], ALU.mult).then_inc(keep_done, 1)
            for k in range(2):
                V.tensor_tensor(kd[k][:, :, :], kd[k][:, :, :], gate[k][:, 1:].unsqueeze(2).to_broadcast([P, BLOCKS, E0]),
                                ALU.mult).then_inc(keep_done, 1)
            dve.wait_ge(keep_done, 9)
            V.tensor_tensor(ck[:, :, :], kd[0][:, :, :], kd[1][:, :, :], ALU.add).then_inc(keep_last, 1)

            def diagonals(k):
                if k >= 2:
                    dve.wait_ge(x1_ps, k - 1)
                for j in range(2):
                    V.tensor_scalar(diag[j][:, k % 2, :], ident, kg[j][:, k:k + 1], None, ALU.mult).then_inc(diag_done, 1)

            def x1_evac(k):
                steps = slice(KCONV - 1 + k * STEPS, KCONV - 1 + (k + 1) * STEPS)
                dve.wait_ge(x1_ps, k + 1)
                V.tensor_tensor(x1p[:, :, steps], bank[k % 2][:, 0:P].rearrange("p (b t) -> p b t", b=B),
                                x_sb[:, k * P:(k + 1) * P].rearrange("p (b t) -> p b t", b=B), ALU.add).then_inc(x1_done, 1)

            def convolve(piece, lo, hi):
                for k in range(KCONV):
                    src, dst = x1p[:, :, k + lo:k + hi], conv[:, :, lo:hi]
                    if k == 0:
                        dve.wait_ge(x1_done, hi // STEPS)
                        o = V.tensor_scalar(dst, src, h0[:, 0:1], cb[:, 0:1], ALU.mult, ALU.add)
                    else:
                        dve.wait_ge(conv_step, piece * KCONV + k)
                        o = V.scalar_tensor_tensor(out=dst, in0=src, scalar=h0[:, k:k + 1], in1=dst, op0=ALU.mult, op1=ALU.add)
                    o.then_inc(conv_step, 1)

            dve.wait_ge(keep_done, 7)
            for e in range(E0):
                for k in range(2):
                    accumulate(last, e, k)
                if e == 0:
                    dve.wait_ge(ckt_ps, 1)
                    V.tensor_copy(ckT[:, :], bank[7][0:BLOCKS * E0, 0:P]).then_inc(ckt_done, 1)
                    diagonals(0)
                if e >= 1:
                    x1_evac(e - 1)
                    diagonals(e)
            dve.wait_ge(in_rec, 16 * N_REC_IN)
            convolve(0, 0, T - STEPS)
            x1_evac(BLOCKS - 1)
            convolve(1, T - STEPS, T)
            dve.wait_ge(sp_act, 4)
            V.tensor_tensor(Bg[:, :], Bg[:, :], Bt[:, :], ALU.add).then_inc(rec, 1)
            dve.wait_ge(rec, 1)
            dve.wait_ge(u_ps, 1)
            V.scalar_tensor_tensor(out=U[:, :], in0=bank[4][:, :], scalar=bs[:, 0:1], in1=Bg[:, :],
                                   op0=ALU.add, op1=ALU.mult).then_inc(rec, 1)
            dve.wait_ge(rec, 2)
            for b in range(2):
                V.tensor_tensor_scan(S[:, b * T:(b + 1) * T], decay_row[:, :], U[:, b * T:(b + 1) * T], 0.0,
                                     ALU.mult, ALU.add).then_inc(rec, 1)
            dve.wait_ge(c_act, 1)
            for b in range(2):
                dve.wait_ge(rec, 3 + b)
                cols = slice(b * T, (b + 1) * T)
                V.scalar_tensor_tensor(out=Yg[:, cols], in0=S[:, cols], scalar=sp_v[:, 1:2], in1=Cg[:, cols],
                                       op0=ALU.mult, op1=ALU.mult).then_inc(rec, 1)

            dve.wait_ge(res_ps, 1)
            for h in range(2):
                V.tensor_copy(acc[:, h * MPG:(h + 1) * MPG, :], bank[6 + h][:, :]).then_inc(res_done, 1)

            def chained(o):
                rt_n[0] += 1
                o.then_inc(rt, 1)
                dve.wait_ge(rt, rt_n[0])

            rt_n = [0]
            dve.wait_ge(rl_ps, 1)
            chained(V.tensor_scalar(pr_e[:, :, :], bank[4][:, 0:TILES * 7].rearrange("p (m e) -> p m e", e=7),
                                    50.0, -50.0, ALU.min, ALU.max))
            dve.wait_ge(e_act, 1)
            chained(V.tensor_scalar(pr_e[:, :, :], pr_e[:, :, :], 1.0, None, ALU.add))
            chained(V.reciprocal(prob[:, :, 0:7], pr_e[:, :, :]))
            for m in range(TILES):
                o = V.max(out=ptop[:, m, :], in_=prob[:, m, :])
            chained(o)
            for m in range(TILES):
                o = V.max_index(out=pidx[:, m, :], in_max=ptop[:, m, :], in_values=prob[:, m, :])
            chained(o)
            V.tensor_copy(pidf[:, :], pidx[:, :, 0])
            chained(V.tensor_scalar(pw[:, :], ptop[:, :, 0], 1e-8, 1.0 - 1e-8, ALU.max, ALU.min))
            chained(V.tensor_scalar(ptw[:, :], pw[:, :], 0.5, 1e-8, ALU.add, ALU.add))
            chained(V.tensor_scalar(ptw[:, :], ptw[:, :], 0.5, 2.0, ALU.max, ALU.min))
            chained(V.reciprocal(prt[:, :], ptw[:, :]))
            chained(V.tensor_tensor(psel[:, :], pw[:, :], prt[:, :], ALU.mult))
            for m in range(TILES):
                o = V.tensor_scalar(wt[:, m, :], iota8[:, :], pidf[:, m:m + 1], psel[:, m:m + 1], ALU.is_equal, ALU.mult)
            chained(o)
            chained(V.tensor_scalar(wt[:, :, 7], prt[:, :], 0.5, None, ALU.mult))

            def gated(k):
                n = IC[k % 3]
                q = k // 3
                dve.wait_ge(g3_ps, k + 1)
                dve.wait_ge(silu_done, k + 1)
                if q >= 2:
                    dve.wait_ge(out_ps, q - 1)
                V.tensor_tensor(hh[0:n, q % 2, k % 3, :], sg[0:n, k % 2, :], bank[k % 2 * 2 + 1][0:n, :],
                                ALU.mult).then_inc(hh_done, 1)

            def add_expert(q):
                g, e = q // E1, q % E1
                dve.wait_ge(out_ps, q + 1)
                for m in range(MPG):
                    M = g * MPG + m
                    if e > 0:
                        dve.wait_ge(acc2, (q - 1) * MPG + m + 1)
                    V.scalar_tensor_tensor(out=acc[:, M, :], in0=bank[6 + q % 2][:, m * P:(m + 1) * P],
                                           scalar=wt[:, M, e:e + 1], in1=acc[:, M, :], op0=ALU.mult,
                                           op1=ALU.add).then_inc(acc2, 1)

            dve.wait_ge(res_done, 2)
            for q in range(2 * E1):
                for c in range(3):
                    gated(3 * q + c)
                if q >= 1:
                    add_expert(q - 1)
            add_expert(2 * E1 - 1)


def kernel(**inputs):
    import numpy as np
    import concourse.bacc as bacc
    from concourse.bass_utils import run_bass_kernel_spmd

    f = {k: np.asarray(v) for k, v in inputs.items()}
    c = lambda v: np.ascontiguousarray(v)
    L0, L1, M0, M1 = "L0_cond_", "L1_cond_", "L0_ffn_", "L1_ffn_"
    col = lambda v: v.reshape(-1, 1)
    tok = np.arange(P)
    b_of, t_of = tok // STEPS, tok % STEPS
    same = b_of[:, None] == b_of[None, :]
    before = same & (t_of[:, None] < t_of[None, :])
    below = b_of[:, None] < b_of[None, :]
    v1 = np.concatenate([f[M1 + "ew1"], f[M1 + "sw1"][None]])
    v3 = np.concatenate([f[M1 + "ew3"], f[M1 + "sw3"][None]])
    v2 = np.concatenate([f[M1 + "ew2"], f[M1 + "sw2"][None]])
    b2 = np.zeros((BLOCKS, E0, BLOCKS, D), np.float32)
    for k in range(BLOCKS):
        b2[k, :, k] = f[M0 + "b2"]
    b2 = b2.reshape(BLOCKS * E0, BLOCKS, D)
    both = lambda v: c(np.concatenate([v, v]))
    arrays = {
        "xT": c(f["x"].reshape(B, BLOCKS, STEPS, D).transpose(3, 1, 0, 2)).reshape(D, BLOCKS * P),
        "gw": c(np.stack([f[L0 + n].T for n in ("Wxr", "Wxz", "Wxh", "Whr", "Whz", "Whh", "Whq")], 1)),
        "gbias": c(np.stack([np.stack([f[L0 + "b" + s + g] for s in "xh"], 1) for g in "rzh"], 1)),
        "qbias": col(f[L0 + "bhq"]),
        "h0": c(f["cond_1024"].T),
        "consts": c(np.stack([np.eye(P), before, same, below], 1).astype(np.float32)),
        "iota8": np.broadcast_to(np.arange(8, dtype=np.float32), (P, 8)).copy(),
        "wg": f[M0 + "Wg"],
        "w1": c(f[M0 + "W1"].transpose(1, 0, 2)),
        "b1": c(f[M0 + "b1"].reshape(E0, HC, P).transpose(2, 0, 1)),
        "w2": c(f[M0 + "W2"].reshape(E0, HC, P, D).transpose(2, 0, 1, 3)),
        "b2": b2,
        "wp": f[L1 + "Wp"], "ws": f[L1 + "Ws"], "wo": both(f[L1 + "Wo"]),
        "cb": col(f[L1 + "conv_b"]), "bpb": both(f[L1 + "bp"].reshape(2, NS).T), "bs": both(col(f[L1 + "bs"])), "bo": col(f[L1 + "bo"]),
        "alog": both(np.stack([f[L1 + "A_log"], f[L1 + "dt_log"]], 1)),
        "rw": c(f[M1 + "router_w"].T), "rb": f[M1 + "routing_bias"].reshape(1, 7),
        "v1": c(v1.transpose(2, 0, 1)), "v3": c(v3.transpose(2, 0, 1)),
        "v2a": c(v2[:, :, :2 * P].reshape(E1, D, 2, P).transpose(3, 0, 2, 1)),
        "v2b": c(v2[:, :, 2 * P:].transpose(2, 0, 1)),
    }
    nc = bacc.Bacc("TRN2", target_bir_lowering=False, num_devices=1)
    args = {k: nc.dram_tensor("in_" + k, v.shape, F32, kind="ExternalInput").ap() for k, v in arrays.items()}
    out = nc.dram_tensor("out", (B * T, D), F32, kind="ExternalOutput").ap()
    adaln_ffn_kernel(nc, args, out)
    r = run_bass_kernel_spmd(nc, [{"in_" + k: v for k, v in arrays.items()}], core_ids=[0])
    return np.asarray(r.results[0]["out"]).reshape(B, T, D)
```

```python
from contextlib import ExitStack

import concourse.bass as bass
from concourse import mybir

F32 = mybir.dt.float32
BF16 = mybir.dt.bfloat16
U32 = mybir.dt.uint32
ALU = mybir.AluOpType
ACT = mybir.ActivationFunctionType
AX_X = mybir.AxisListType.X

P = 128
B, T, D = 4, 256, 128
STEPS = 32
BLOCKS = T // STEPS
SLOTS = BLOCKS + 1
E0, H0 = 8, 512
HC = H0 // P
CAP = -(-B * T * 2 * 105 // (E0 * 100))
NS = 64
KCONV = 4
E1, I1 = 8, 352
IC1 = -(-I1 // P)
WARM_A, WARM_B = 480, 480
WARM_FIRST = 512
WARM_UP = 8
WARM_REC = (5, 14, 4)
TILES = B * T // P
SORTED = TILES + E1 - 2
CONV = ((0, 64), (64, 128), (128, 192), (192, 224), (224, 256))
HEAD = 192
GRP = 512
MPG = GRP // P


def adaln_ffn_kernel(nc, a, out):
    with ExitStack() as ctx:
        def sb(name, shape, dt=F32):
            return ctx.enter_context(nc.sbuf_tensor(name, shape, dt))

        def psum(name):
            return ctx.enter_context(nc.psum_tensor(name, [P, 512], F32))

        def sem(name):
            return ctx.enter_context(nc.semaphore(name))

        small = sb("small", [P, 11 + P + BLOCKS * P])
        gbias = small[:, 0:6].rearrange("p (g s) -> p g s", s=2)
        qbias = small[:, 6:7]
        h0 = small[:, 7:11]
        ident = small[:, 11:11 + P]
        x_sb = small[:, 11 + P:]
        gw = sb("gw", [P, 7, P])
        consts = sb("consts", [P, 3, P])
        iota16 = sb("iota16", [P, 16])
        iota8 = iota16[:, 0:8]
        wg = sb("wg", [P, E0])
        w1 = sb("w1", [P, E0, H0])
        b1 = sb("b1", [P, E0, HC])
        w2 = sb("w2", [P, E0, HC, D])
        b2 = sb("b2", [BLOCKS * E0, BLOCKS, D])
        m_before, m_same, m_below = (consts[:, k, :] for k in range(3))

        gws = sb("gws", [P, 5, P])
        wr_q, wr_p, wz_g, wh_rh, wq_g = (gws[:, k, :] for k in range(5))
        gb = sb("gb", [P, 3])
        xp = sb("xp", [P, 3, (BLOCKS + 1) * P])
        G = sb("G", [P, B, STEPS])
        Q4 = sb("Q4", [P, B])
        P2 = sb("P2", [P, B])
        RH4 = sb("RH4", [P, B])
        tr = sb("tr", [P, B])
        tz = sb("tz", [P, B])
        ht = sb("ht", [P, B])
        yT = sb("yT", [P, P])
        hT = [sb("hT%d" % k, [P, HC, P]) for k in range(2)]
        warm = sb("warm", [P, 512], BF16)
        lg = sb("lg", [P, E0])
        top8 = sb("top8", [P, 8])
        idx8 = sb("idx8", [P, 8], U32)
        idxf = sb("idxf", [P, 2])
        gap = sb("gap", [P, 1])
        tgap = sb("tgap", [P, 1])
        gate = [sb("gate%d" % k, [P, SLOTS]) for k in range(2)]
        oh = [sb("oh%d" % k, [P, SLOTS, E0]) for k in range(2)]
        oh_cur = [sb("oh_cur%d" % k, [P, E0]) for k in range(2)]
        A_cur = [sb("A_cur%d" % k, [P, D]) for k in range(2)]
        cnt = sb("cnt", [P, SLOTS, E0])
        A = [sb("A%d" % k, [P, SLOTS, D]) for k in range(2)]

        pref = sb("pref", [P, SLOTS + 1, E0])
        kept = sb("kept", [P, BLOCKS, E0])
        kd = [sb("kd%d" % k, [P, BLOCKS, E0]) for k in range(2)]
        ck = sb("ck", [P, BLOCKS, E0])
        ckT = sb("ckT", [BLOCKS * E0, P])
        kg = [sb("kg%d" % k, [P, BLOCKS]) for k in range(2)]
        diag = [sb("diag%d" % k, [P, P]) for k in range(2)]
        x1p = sb("x1p", [P, B, KCONV - 1 + T])

        wp = sb("wp", [P, 2 * NS])
        ws = sb("ws", [P, NS])
        wo = sb("wo", [P, D])
        cb = sb("cb", [P, 1])
        bpb = sb("bpb", [P, 2])
        bs = sb("bs", [P, 1])
        bo = sb("bo", [P, 1])
        alog = sb("alog", [P, 2])
        sp_t = sb("sp_t", [P, 2])
        sp_r = sb("sp_r", [P, 2])
        sp_v = sb("sp_v", [P, 2])
        decay = sb("decay", [P, 1])
        decay_row = sb("decay_row", [P, T])
        conv = sb("conv", [P, B, T])
        Cg = sb("Cg", [P, GRP])
        Bg = sb("Bg", [P, GRP])
        Bt = sb("Bt", [P, GRP])
        U = sb("U", [P, GRP])
        S = sb("S", [P, GRP])
        Yg = sb("Yg", [P, GRP])
        xc = sb("xc", [P, B * T])

        rw = sb("rw", [P, 7])
        rb = sb("rb", [P, 7])
        v1 = sb("v1", [P, E1, IC1 * P])
        v3 = sb("v3", [P, E1, IC1 * P])
        v2 = sb("v2", [P, E1, IC1, D])
        ones8 = sb("ones8", [P, 8])
        sortc = sb("sortc", [P, 3 * P + 1])
        earlier, iota128 = sortc[:, 0:P], sortc[:, P:2 * P]
        firsts = sortc[:, 2 * P:2 * P + 16]
        trash = sortc[:, 2 * P + 16:2 * P + 16 + SORTED]
        part = sortc[:, 3 * P:3 * P + 1]
        earlier_bf = sb("earlier_bf", [P, P], BF16)
        prob = sb("prob", [P, TILES, 8])
        pr_e = sb("pr_e", [P, TILES, 7])
        ptop = sb("ptop", [P, TILES, 8])
        pidx = sb("pidx", [P, TILES, 8], U32)
        pidf = sb("pidf", [P, TILES])
        chosen = sb("chosen", [P, TILES, 8], BF16)
        over = sb("over", [P, 8, 8])
        blocks_of = sb("blocks_of", [P, 8])
        blocks_to = sb("blocks_to", [P, 8])
        base = sb("base", [P, 8])
        place = sb("place", [P, TILES, 8])
        row_f = sb("row_f", [P, TILES])
        above = sb("above", [P, TILES, 16])
        blk1 = sb("blk1", [P, TILES, SORTED])
        blk_f = sb("blk_f", [P, TILES])
        lane = sb("lane", [P, TILES])
        lane1 = sb("lane1", [P, TILES, P], BF16)
        token2 = sb("token2", [P, TILES, 2, SORTED], BF16)
        token_t = sb("token_t", [P, SORTED])
        missing = sb("missing", [P, SORTED])
        source = sb("source", [P, SORTED], U32)
        target = sb("target", [P, SORTED], U32)
        passed = sb("passed", [1, SORTED, 8])
        block_expert_f = sb("block_expert_f", [1, SORTED])
        block_expert = sb("block_expert", [1, SORTED], U32)
        pw = sb("pw", [P, TILES])
        ptw = sb("ptw", [P, TILES])
        prt = sb("prt", [P, TILES])
        pshared = sb("pshared", [P, TILES])
        sg = sb("sg", [P, 2, GRP])
        hh = sb("hh", [P, 2, IC1, GRP])
        xct = sb("xct", [P, TILES, D + 1])
        psel = xct[:, :, D]
        vb = sb("vb", [P, 2, 2, IC1 * P])
        xs = sb("xs", [P, SORTED, D + 1])
        xsT = sb("xsT", [P, 2, P])
        ys = sb("ys", [P, SORTED, D])
        zeros = ys[:, :, :]
        acc = sb("acc", [P, TILES, D])
        xc_dram = nc.dram_tensor("xc_rows", (B * T, D + 1), F32, kind="Internal").ap()

        bank = [psum("bank%d" % k) for k in range(8)]
        pre = [bank[g][:, 0:P].rearrange("p (b t) -> p b t", b=B) for g in range(3)]
        ps_h = [bank[3 + k][:, :].rearrange("p (c t) -> p c t", c=HC) for k in range(2)]
        ps_y = bank[5][:, 0:D]
        ps_y2 = (ps_y, bank[2][:, 0:D])
        ps_misc = bank[6]
        ps_warm = bank[7][:, :]

        in_gru, in_x, warm_set, in_moe, in_rec, in_l1 = sem("in_gru"), sem("in_x"), sem("warm_set"), sem("in_moe"), sem("in_rec"), sem("in_l1")
        pool_set = sem("pool_set")
        weights_scaled, gbias_sum = sem("weights_scaled"), sem("gbias_sum")
        xp_ps, xp_done = sem("xp_ps"), sem("xp_done")
        r_pre, z_pre, h_pre = sem("r_pre"), sem("z_pre"), sem("h_pre")
        r_act, z_act, h_act = sem("r_act"), sem("z_act"), sem("h_act")
        rh_rdy, q_rdy, p_rdy, g_rdy = sem("rh_rdy"), sem("q_rdy"), sem("p_rdy"), sem("g_rdy")
        yt_ps, yt_done, lg_ps, route, gap_act = sem("yt_ps"), sem("yt_done"), sem("lg_ps"), sem("route"), sem("gap_act")
        up_ps, gelu_done, down_ps, acc_done = sem("up_ps"), sem("gelu_done"), sem("down_ps"), sem("acc_done")
        pref_done, pos_ps, keep_done = sem("pref_done"), sem("pos_ps"), sem("keep_done")
        diag_done, x1_ps, x1_done = sem("diag_done"), sem("x1_ps"), sem("x1_done")
        ckt_ps, ckt_done, conv_step, keep_last = sem("ckt_ps"), sem("ckt_done"), sem("conv_step"), sem("keep_last")
        mix, relu_done = sem("mix"), sem("relu_done")
        dec_act, dec_dve = sem("dec_act"), sem("dec_dve")
        cproj_ps, bproj_ps, u_ps = sem("cproj_ps"), sem("bproj_ps"), sem("u_ps")
        sp_act, c_act, rec = sem("sp_act"), sem("c_act"), sem("rec")
        xc_ps, xc_done = sem("xc_ps"), sem("xc_done")
        rl_ps, rt, e_act = sem("rl_ps"), sem("rt"), sem("e_act")
        res_ps, res_done = sem("res_ps"), sem("res_done")
        g1_ps, g3_ps, silu_done, hh_done, out_ps, acc2 = (sem("g1_ps"), sem("g3_ps"), sem("silu_done"),
                                                         sem("hh_done"), sem("out_ps"), sem("acc2"))
        xct_ps, xct_done, chosen_done = sem("xct_ps"), sem("xct_done"), sem("chosen_done")
        place_ps, sort_in, token_ps, rows_known = sem("place_ps"), sem("sort_in"), sem("token_ps"), sem("rows_known")
        expert_known = sem("expert_known")
        xc_stored, xst_ps, xst_done = sem("xc_stored"), sem("xst_ps"), sem("xst_done")
        xs_loaded = [sem("xs_loaded%d" % q) for q in range(SORTED)]
        s1_ps, s3_ps, s_silu, s_hh, s_out, ys_done = (sem("s1_ps"), sem("s3_ps"), sem("s_silu"), sem("s_hh"),
                                                      sem("s_out"), sem("ys_done"))
        vb1_done, vb3_done = sem("vb1_done"), sem("vb3_done")
        returned, psel_done = sem("returned"), sem("psel_done")
        stored = sem("stored")

        def up_cnt(s, e):
            return 8 * (s - 1) + e + 2

        def gelu_cnt(s, e):
            return 8 * (s - 1) + e + 3

        def down_cnt(s, e):
            return 8 * (s - 1) + e + 4

        N_ROUTE = 8
        N_GRU_IN, N_MOE_IN, N_REC_IN, N_L1_IN = 2, 7, 9, 5

        block = ctx.enter_context(nc.Block())

        @block.sync
        def _(sp):
            first = 11 + 2 * P
            sp.dma_start(gw[:, :, :], a["gw"]).then_inc(in_gru, 16)
            sp.dma_start(small[:, 0:first], a["small"][:, 0:first]).then_inc(in_gru, 16)
            sp.dma_start(small[:, first:], a["small"][:, first:]).then_inc(in_x, 16)
            for dst, src in ((w1[:, :, :], "w1"), (wg[:, :], "wg"), (b1[:, :, :], "b1"), (w2[:, :, :, :], "w2"),
                             (b2[:, :, :], "b2"), (iota16[:, :], "iota16"), (consts[:, :, :], "consts")):
                sp.dma_start(dst, a[src]).then_inc(in_moe, 16)
            for dst, src in ((wp[:, :], "wp"), (ws[:, :], "ws"), (wo[:, :], "wo"), (cb[:, :], "cb"),
                             (bpb[:, :], "bpb"), (bs[:, :], "bs"), (bo[:, :], "bo"), (rw[:, :], "rw"), (alog[:, :], "alog")):
                sp.dma_start(dst, a[src]).then_inc(in_rec, 16)
            for dst, src in ((rb[:, :], "rb"), (v1[:, :, :], "v1"), (v3[:, :, :], "v3"),
                             (v2[:, :, :, :], "v2"), (sortc[:, :], "sortc")):
                sp.dma_start(dst, a[src]).then_inc(in_l1, 16)
            sp.wait_ge(pool_set, 1)
            sp.dma_start(out[B * T:, :].rearrange("(j p) d -> p j d", p=P), zeros).then_inc(stored, 16)
            sp.wait_ge(xct_done, 2)
            sp.wait_ge(psel_done, 1)
            sp.dma_start(xc_dram.rearrange("(m p) d -> p m d", p=P), xct[:, :, :]).then_inc(xc_stored, 16)
            for g in range(2):
                sp.wait_ge(acc2, MPG * (g + 1))
                sp.dma_start(out[g * GRP:(g + 1) * GRP, :].rearrange("(m p) d -> p m d", p=P),
                             acc[:, g * MPG:(g + 1) * MPG, :]).then_inc(stored, 16)
            sp.wait_ge(stored, 48)
            sp.wait_ge(returned, 16 * SORTED)

        @block.gpsimd
        def _(pool):
            nc.gpsimd.memset(warm[:, :], 1.0).then_inc(warm_set, 1)
            nc.gpsimd.memset(xp[:, :, BLOCKS * P:], 0.0)
            nc.gpsimd.memset(x1p[:, :, 0:KCONV - 1], 0.0)
            nc.gpsimd.memset(hT[0][:, :, :], 0.0)
            nc.gpsimd.memset(hT[1][:, :, :], 0.0).then_inc(gelu_done, 1)
            nc.gpsimd.memset(oh_cur[0][:, :], 0.0)
            nc.gpsimd.memset(oh_cur[1][:, :], 0.0)
            nc.gpsimd.memset(A_cur[0][:, :], 0.0)
            nc.gpsimd.memset(A_cur[1][:, :], 0.0).then_inc(down_ps, 1)
            nc.gpsimd.memset(prob[:, :, :], -1.0)
            nc.gpsimd.memset(ones8[:, :], 1.0)
            nc.gpsimd.memset(vb[:, :, :, I1:], 0.0)
            nc.gpsimd.memset(zeros, 0.0)
            nc.gpsimd.memset(pref[:, 0:2, :], 0.0).then_inc(pool_set, 1)
            pool.wait_ge(keep_done, 7)
            for k in range(BLOCKS - 1):
                for c in range(2):
                    o = A[c][:, k + 1, :]
                    nc.gpsimd.tensor_scalar(o, o, kg[c][:, k:k + 1], None, ALU.mult).then_inc(mix, 1)
                pool.wait_ge(mix, 3 * k + 2)
                nc.gpsimd.tensor_tensor(A[0][:, k + 1, :], A[0][:, k + 1, :], A[1][:, k + 1, :], ALU.add).then_inc(mix, 1)
            pool.wait_ge(xc_stored, 16)
            pool.wait_ge(rows_known, 1)
            for j in range(SORTED):
                nc.gpsimd.indirect_dma_start(out=xs[:, j, :], out_offset=None, in_=xc_dram,
                                             in_offset=bass.IndirectOffsetOnAxis(source[:, j:j + 1], 0))\
                    .then_inc(xs_loaded[j], 16)
            pool.wait_ge(rows_known, 2)
            pool.wait_ge(stored, 48)
            for j in range(SORTED):
                pool.wait_ge(ys_done, j + 1)
                nc.gpsimd.indirect_dma_start(out=out, compute_op=ALU.add, out_offset=bass.IndirectOffsetOnAxis(target[:, j:j + 1], 0),
                                             in_=ys[:, j, :], in_offset=None).then_inc(returned, 16)

        @block.tensor
        def _(pe):
            def mm(o, lhsT, rhs, start=False, stop=False):
                return nc.tensor.matmul(o, lhsT, rhs, start=start, stop=stop, skip_group_check=True)

            def transpose(o, x, start=True):
                return nc.tensor.matmul(o, x, ident, start=start, stop=True, is_transpose=True, skip_group_check=True)

            def keep_warm(n):
                mm(ps_warm[:, 0:n], warm[:, 0:P], warm[:, 0:n], start=True, stop=True)

            def x_products(i):
                pe.wait_ge(in_x, 16)
                if i >= 2:
                    pe.wait_ge(xp_done, i - 1)
                for g in range(3):
                    last = mm(ps_misc[:, g * P:(g + 1) * P], gw[:, g, :], x_sb[:, i * P:(i + 1) * P],
                              start=(g == 0), stop=True)
                last.then_inc(xp_ps, 1)

            def inject(g, i):
                return mm(bank[g][:, 0:P], ident, xp[:, g, bass.ds(i * P, P)], start=True)

            def inject_first(g):
                mm(bank[g][:, 0:P], gw[:, g, :], x_sb[:, 0:P], start=True)
                mm(bank[g][:, 0:P], ident, gb[:, g:g + 1].to_broadcast([P, P]))

            def y_product(i):
                pe.wait_ge(g_rdy, i * STEPS + 1)
                mm(ps_misc[:, 0:P], wq_g, G[:, :, :].rearrange("p b t -> p (b t)"), start=True, stop=True)\
                    .then_inc(yt_ps, 1)

            def router_product(s):
                pe.wait_ge(yt_done, s)
                mm(ps_misc[:, 0:E0], yT[:, :], wg[:, :], start=True, stop=True).then_inc(lg_ps, 1)

            def up(s, e, c):
                if c == 0:
                    pe.wait_ge(gelu_done, gelu_cnt(s, e - 2))
                    if e == 0:
                        pe.wait_ge(yt_done, s)
                m = mm(ps_h[e % 2][:, c, :], w1[:, e, c * P:(c + 1) * P], yT[:, :], start=(c == 0), stop=True)
                if c == HC - 1:
                    m.then_inc(up_ps, 1)

            def down(s, e, c, o=ps_y, behind=1):
                if c == 0:
                    pe.wait_ge(gelu_done, gelu_cnt(s, e))
                    pe.wait_ge(acc_done, down_cnt(s, e - behind))
                m = mm(o, hT[e % 2][:, c, :], w2[:, e, c, :], start=(c == 0), stop=(c == HC - 1))
                if c == HC - 1:
                    m.then_inc(down_ps, 1)

            def side(i, t, half):
                if t % 4 in (2, 3):
                    up(i, t // 4, (t % 4 - 2) * 2 + half)
                else:
                    e = t // 4 - 2
                    down(i if e >= 0 else i - 1, e % E0, (t % 4) * 2 + half)
                if (t, half) == (1, 1):
                    router_product(i)

            def first_side(i, t, half):
                keep_warm(WARM_FIRST)
                if half == 1 and t % 4 == 1 and t // 4 + 1 < BLOCKS:
                    x_products(t // 4 + 1)

            def gru_block(i, side):
                for t in range(STEPS):
                    n = i * STEPS + t
                    pe.wait_ge(q_rdy, n + 1)
                    mm(pre[0][:, :, t], wr_q, Q4[:, :])
                    pe.wait_ge(p_rdy, n + 1)
                    mm(pre[0][:, :, t], wr_p, P2[:, :]).then_inc(r_pre, 1)
                    if t == 0:
                        inject_first(2) if side is first_side else inject(2, i)
                    else:
                        side(i, t, 0)
                    pe.wait_ge(g_rdy, n + 1)
                    mm(pre[1][:, :, t], wz_g, G[:, :, (t - 1) % STEPS]).then_inc(z_pre, 1)
                    if t == 0 and side is not first_side:
                        y_product(i)
                    elif t == STEPS - 1:
                        pe.wait_ge(r_act, n + 1)
                        inject(0, i + 1)
                    else:
                        keep_warm(WARM_A)
                    pe.wait_ge(rh_rdy, n + 1)
                    mm(pre[2][:, :, t], wh_rh, RH4[:, :], stop=True).then_inc(h_pre, 1)
                    if t == 0:
                        side(i, 0, 0)
                    side(i, t, 1)
                    if t == STEPS - 1:
                        pe.wait_ge(z_act, n + 1)
                        inject(1, i + 1)
                    elif t not in (0, 1):
                        keep_warm(WARM_B)

            pe.wait_ge(warm_set, 1)
            for _ in range(WARM_UP):
                keep_warm(512)
            pe.wait_ge(in_gru, 16 * N_GRU_IN)
            pe.wait_ge(gbias_sum, 1)
            inject_first(0)
            inject_first(1)
            pe.wait_ge(weights_scaled, 5)
            gru_block(0, first_side)
            pe.wait_ge(in_moe, 16 * N_MOE_IN)
            pe.wait_ge(pool_set, 1)
            with pe.Fori(1, BLOCKS) as i:
                gru_block(i, side)

            last_slot = SLOTS - 1
            y_product(BLOCKS)
            for c in range(HC):
                down(last_slot - 1, 6, c)
            router_product(last_slot)
            for c in range(HC):
                down(last_slot - 1, 7, c, ps_y2[1], 2)

            def positions():
                pe.wait_ge(pref_done, BLOCKS)
                o = ps_misc[:, 0:BLOCKS * E0]
                mm(o, m_before, cnt[:, 1:, :], start=True)
                mm(o, m_same, pref[:, 1:SLOTS, :])
                mm(o, m_below, pref[:, SLOTS:SLOTS + 1, :].to_broadcast([P, BLOCKS, E0]), stop=True).then_inc(pos_ps, 1)

            def x1_product(k):
                if k >= 2:
                    pe.wait_ge(x1_done, k - 1)
                o = bank[k % 2][:, 0:P]
                if k < BLOCKS - 1:
                    pe.wait_ge(mix, 3 * k + 3)
                    transpose(o, A[0][:, k + 1, :])
                else:
                    pe.wait_ge(diag_done, 2)
                    pe.wait_ge(acc_done, down_cnt(last_slot, E0 - 1))
                    mm(o, A[0][:, k + 1, :], diag[0][:, :], start=True)
                    mm(o, A[1][:, k + 1, :], diag[1][:, :])
                mm(o, b2[:, k, :], ckT[:, :], stop=True).then_inc(x1_ps, 1)

            for e in range(E0 + 2):
                if e < E0:
                    for c in range(HC):
                        up(last_slot, e, c)
                if e == 1:
                    positions()
                if e >= 2:
                    for c in range(HC):
                        down(last_slot, e - 2, c, ps_y2[e % 2], 2)
                if e == 2:
                    pe.wait_ge(keep_last, 1)
                    mm(bank[7][0:BLOCKS * E0, 0:P], ck[:, :, :].rearrange("p k e -> p (k e)"), ident, start=True, stop=True)\
                        .then_inc(ckt_ps, 1)
                if e == 3:
                    pe.wait_ge(ckt_done, 1)
                if 3 <= e:
                    x1_product(e - 3)

            pe.wait_ge(in_rec, 16 * N_REC_IN)

            def project(o, w, source, lo, hi):
                for g in range(2):
                    last = mm(o[NS * g:NS * (g + 1), :].rearrange("p (b t) -> p b t", b=2)[:, :, lo:hi], w,
                              source[:, 2 * g:2 * g + 2, lo:hi], start=(lo == 0), stop=True)
                return last

            def stay_warm(k):
                for _ in range(WARM_REC[k]):
                    mm(bank[5][:, :], warm[:, 0:P], warm[:, :], start=True, stop=True)

            x1_steps = x1p[:, :, KCONV - 1:]
            pe.wait_ge(x1_done, HEAD // STEPS)
            project(bank[7], ws[:, :], x1_steps, 0, HEAD)
            stay_warm(0)
            x1_product(BLOCKS - 1)
            pe.wait_ge(conv_step, 3 * KCONV)
            project(bank[6], wp[:, 0:NS], conv, 0, HEAD)
            project(bank[2], wp[:, NS:], conv, 0, HEAD)
            pe.wait_ge(conv_step, 5 * KCONV)
            project(bank[6], wp[:, 0:NS], conv, HEAD, T).then_inc(bproj_ps, 1)
            project(bank[7], ws[:, :], x1_steps, HEAD, T).then_inc(u_ps, 1)
            project(bank[2], wp[:, NS:], conv, HEAD, T).then_inc(cproj_ps, 1)
            pe.wait_ge(in_l1, 16 * N_L1_IN)
            for m in range(TILES):
                b, h = m // 2, m % 2
                last = mm(bank[3 + m // 4][:, (m % 4) * P:(m % 4 + 1) * P],
                          x1p[:, b, KCONV - 1 + h * P:KCONV - 1 + (h + 1) * P], ident, start=(m % 4 == 0), stop=True)
            last.then_inc(res_ps, 1)
            stay_warm(1)
            for g in range(2):
                if g == 0:
                    pe.wait_ge(rec, 6)
                rows = slice(NS * g, NS * (g + 1))
                mm(bank[g][:, :], wo[rows, :], Yg[rows, :], start=True, stop=True).then_inc(xc_ps, 1)
            stay_warm(2)
            pe.wait_ge(xc_done, 2)
            pe.wait_ge(res_done, 2)
            for m in range(TILES):
                last = mm(bank[4][:, m * 7:(m + 1) * 7], xc[:, m * P:(m + 1) * P], rw[:, :], start=(m == 0), stop=True)
            last.then_inc(rl_ps, 1)

            for m in range(TILES):
                last = transpose(bank[2 + m // 4][:, m % 4 * P:(m % 4 + 1) * P], xc[:, m * P:(m + 1) * P], m % 4 == 0)
                if m % 4 == 3:
                    last.then_inc(xct_ps, 1)

            def ups(g, c):
                k = g * IC1 + c
                cols = slice(c * P, (c + 1) * P)
                rhs = xc[:, g * GRP:(g + 1) * GRP]
                if k == 1:
                    pe.wait_ge(xct_done, 2)
                if k >= 2:
                    pe.wait_ge(hh_done, k - 1)
                mm(bank[k % 2 * 2][:, :], v1[:, E1 - 1, cols], rhs, start=True, stop=True).then_inc(g1_ps, 1)
                mm(bank[k % 2 * 2 + 1][:, :], v3[:, E1 - 1, cols], rhs, start=True, stop=True).then_inc(g3_ps, 1)

            def outs(g, lo, hi):
                for c in range(lo, hi):
                    pe.wait_ge(hh_done, IC1 * g + c + 1)
                    for m in range(MPG):
                        last = mm(bank[6 + g][:, m * P:(m + 1) * P], hh[:, g, c, m * P:(m + 1) * P], v2[:, E1 - 1, c, :],
                                  start=(m == 0 and c == 0), stop=(c == IC1 - 1))
                if hi == IC1:
                    last.then_inc(out_ps, 1)

            def places():
                o = bank[5][:, 0:(TILES + 1) * 8].rearrange("p (m e) -> p m e", e=8)
                pe.wait_ge(chosen_done, 1)
                mm(o[:, 0:TILES, :], earlier_bf[:, :], chosen[:, :, :], start=True)
                for m in range(TILES):
                    last = mm(o[:, m + 1:, :], warm[:, 0:P], chosen[:, m:m + 1, :].to_broadcast([P, TILES - m, 8]),
                              stop=(m == TILES - 1))
                last.then_inc(place_ps, 1)

            def row_tokens():
                pe.wait_ge(sort_in, 1)
                for m in range(TILES):
                    last = mm(bank[5][:, P:P + 2 * SORTED], lane1[:, m, :], token2[:, m, :, :], start=(m == 0),
                              stop=(m == TILES - 1))
                last.then_inc(token_ps, 1)

            ups(0, 0)
            ups(0, 1)
            places()
            ups(0, 2)
            ups(1, 0)
            outs(0, 0, IC1)
            ups(1, 1)
            row_tokens()
            ups(1, 2)
            outs(1, 0, IC1 - 1)

            def turn(j):
                pe.wait_ge(xs_loaded[j], 16)
                if j >= 2:
                    pe.wait_ge(xst_done, j - 1)
                transpose(bank[4 + j % 2][:, 0:P], xs[:, j, 0:D]).then_inc(xst_ps, 1)

            def sorted_ups(j):
                x_block = xsT[:, j % 2, :]
                if j < 2:
                    pe.wait_ge(hh_done, 2 * IC1)
                else:
                    pe.wait_ge(s_hh, j - 1)
                for k, (vb_done, s_ps) in enumerate(((vb1_done, s1_ps), (vb3_done, s3_ps))):
                    pe.wait_ge(vb_done, j + 1)
                    for c in range(IC1):
                        last = mm(bank[j % 2 * 2 + k][:, c * P:(c + 1) * P],
                                  vb[:, j % 2, k, c * P:(c + 1) * P], x_block,
                                  start=(c == 0), stop=True)
                    last.then_inc(s_ps, 1)

            def sorted_out(j):
                if j < 2:
                    pe.wait_ge(acc2, MPG * (j + 1))
                else:
                    pe.wait_ge(ys_done, j - 1)
                pe.wait_ge(s_hh, j + 1)
                expert = pe.value_load(block_expert[0:1, j:j + 1], min_val=0, max_val=E1 - 2)
                for c in range(IC1):
                    last = mm(bank[6 + j % 2][:, 0:P], hh[:, j % 2, c, 0:P],
                              v2[:, bass.ds(expert, 1), c, :].rearrange("p a d -> p (a d)"),
                              start=(c == 0), stop=(c == IC1 - 1))
                last.then_inc(s_out, 1)

            turn(0)
            outs(1, IC1 - 1, IC1)
            turn(1)
            pe.wait_ge(expert_known, 1)
            for j in range(SORTED + 1):
                if j < SORTED:
                    pe.wait_ge(xst_done, j + 1)
                    sorted_ups(j)
                if j + 2 < SORTED:
                    turn(j + 2)
                if j >= 1:
                    sorted_out(j - 1)

        @block.scalar
        def _(act):
            nc.scalar.preload_act_table_set("gelu_apprx_tanh_and_others")

            def xp_evac(g, k):
                o = nc.scalar.activation(xp[:, g, k * P:(k + 1) * P], ps_misc[:, g * P:(g + 1) * P], ACT.Identity,
                                         bias=gb[:, g:g + 1])
                if g == 2:
                    o.then_inc(xp_done, 1)

            def gelu(s, e, c, in_loop=False):
                if c == 0:
                    act.wait_ge(up_ps, up_cnt(s, e))
                    if not in_loop:
                        act.wait_ge(down_ps, down_cnt(s, e - 2))
                g = nc.scalar.activation(hT[e % 2][:, c, :], ps_h[e % 2][:, c, :], ACT.Gelu_apprx_tanh,
                                         bias=b1[:, e, c:c + 1])
                if c == HC - 1:
                    g.then_inc(gelu_done, 1)

            def gap_tanh(s):
                act.wait_ge(route, N_ROUTE * (s - 1) + 2)
                nc.scalar.activation(tgap[:, :], gap[:, :], ACT.Tanh, scale=0.5).then_inc(gap_act, 1)

            act.wait_ge(gbias_sum, 1)

            def side(i, t):
                e = t // 4 - 1
                gelu(i if e >= 0 else i - 1, e % E0, t % 4, in_loop=True)

            def late_side(i, t):
                if t == 8:
                    gap_tanh(i)

            def first_side(i, t):
                k = t // 4 + 1
                if t % 4 == 3 and k < BLOCKS:
                    act.wait_ge(xp_ps, k)
                    for g in range(3):
                        xp_evac(g, k)

            def gru_block(i, side, late_side):
                for t in range(STEPS):
                    n = i * STEPS + t
                    act.wait_ge(r_pre, n + 1)
                    nc.scalar.activation(tr[:, :], pre[0][:, :, t], ACT.Tanh, scale=0.5).then_inc(r_act, 1)
                    side(i, t)
                    act.wait_ge(z_pre, n + 1)
                    nc.scalar.activation(tz[:, :], pre[1][:, :, t], ACT.Tanh, scale=0.5).then_inc(z_act, 1)
                    act.wait_ge(h_pre, n + 1)
                    nc.scalar.activation(ht[:, :], pre[2][:, :, t], ACT.Tanh).then_inc(h_act, 1)
                    late_side(i, t)

            gru_block(0, first_side, lambda i, t: None)
            act.wait_ge(in_moe, 16 * N_MOE_IN)
            act.wait_ge(pool_set, 1)
            with act.Fori(1, BLOCKS) as i:
                gru_block(i, side, late_side)
            for c in range(HC):
                gelu(SLOTS - 2, 7, c)
            for e in range(E0):
                for c in range(HC):
                    gelu(SLOTS - 1, e, c)
                if e == 0:
                    gap_tanh(SLOTS - 1)

            nc.scalar.preload_act_table_set("natural_log_exp_and_others")
            act.wait_ge(in_rec, 16 * N_REC_IN)
            nc.scalar.activation(sp_t[:, :], alog[:, :], ACT.Abs).then_inc(dec_act, 1)
            act.wait_ge(dec_act, 1)
            nc.scalar.activation(sp_t[:, :], sp_t[:, :], ACT.Exp, scale=-1.0).then_inc(dec_act, 1)
            act.wait_ge(dec_act, 2)
            nc.scalar.activation(sp_t[:, :], sp_t[:, :], ACT.Ln, bias=1.0).then_inc(dec_act, 1)
            nc.scalar.activation(sp_r[:, :], alog[:, :], ACT.Relu).then_inc(dec_act, 1)
            act.wait_ge(bproj_ps, 1)
            nc.scalar.activation(Bt[:, :], bank[6][:, :], ACT.Abs, bias=bpb[:, 0:1]).then_inc(sp_act, 1)
            act.wait_ge(sp_act, 1)
            nc.scalar.activation(Bt[:, :], Bt[:, :], ACT.Exp, scale=-1.0).then_inc(sp_act, 1)
            act.wait_ge(sp_act, 2)
            nc.scalar.activation(Bt[:, :], Bt[:, :], ACT.Ln, bias=1.0).then_inc(sp_act, 1)
            nc.scalar.preload_act_table_set("exp_and_others")
            act.wait_ge(cproj_ps, 1)
            nc.scalar.activation(Cg[:, :], bank[2][:, :], ACT.Tanh, bias=bpb[:, 1:2]).then_inc(c_act, 1)
            act.wait_ge(res_ps, 1)
            for h in range(2):
                nc.scalar.activation(acc[:, h * MPG:(h + 1) * MPG, :], bank[3 + h][:, :], ACT.Identity).then_inc(res_done, 1)
            for g in range(2):
                act.wait_ge(xc_ps, g + 1)
                nc.scalar.activation(xc[:, g * GRP:(g + 1) * GRP], bank[g][:, :], ACT.Identity,
                                     bias=bo[:, 0:1]).then_inc(xc_done, 1)
            act.wait_ge(rt, 2)
            nc.scalar.activation(pr_e[:, :, :], pr_e[:, :, :], ACT.Exp, scale=-1.0).then_inc(e_act, 1)
            nc.scalar.preload_act_table_set("silu_and_others")
            for h in range(2):
                act.wait_ge(xct_ps, h + 1)
                nc.scalar.activation(xct[:, h * MPG:(h + 1) * MPG, 0:D],
                                     bank[2 + h][:, :].rearrange("p (m d) -> p m d", d=D), ACT.Identity).then_inc(xct_done, 1)
            for k in range(2 * IC1):
                act.wait_ge(g1_ps, k + 1)
                if k >= 2:
                    act.wait_ge(hh_done, k - 1)
                nc.scalar.activation(sg[:, k % 2, :], bank[k % 2 * 2][:, :], ACT.Silu).then_inc(silu_done, 1)
            def own_v3(j):
                if j == 0:
                    act.wait_ge(expert_known, 1)
                if j >= 2:
                    act.wait_ge(s3_ps, j - 1)
                expert = act.value_load(block_expert[0:1, j:j + 1], min_val=0, max_val=E1 - 2)
                nc.scalar.activation(vb[:, j % 2, 1, 0:I1].unsqueeze(1), v3[:, bass.ds(expert, 1), 0:I1], ACT.Identity)\
                    .then_inc(vb3_done, 1)

            own_v3(0)
            for j in range(SORTED):
                act.wait_ge(xst_ps, j + 1)
                if j >= 2:
                    act.wait_ge(s3_ps, j - 1)
                nc.scalar.activation(xsT[:, j % 2, :], bank[4 + j % 2][:, 0:P], ACT.Identity).then_inc(xst_done, 1)
                if j + 1 < SORTED:
                    own_v3(j + 1)
                act.wait_ge(s1_ps, j + 1)
                if j < 2:
                    act.wait_ge(hh_done, 2 * IC1)
                else:
                    act.wait_ge(s_hh, j - 1)
                nc.scalar.activation(sg[:, j % 2, 0:IC1 * P], bank[j % 2 * 2][:, 0:IC1 * P], ACT.Silu).then_inc(s_silu, 1)

        @block.vector
        def _(dve):
            V = nc.vector
            dve.wait_ge(in_gru, 16 * N_GRU_IN)
            V.tensor_tensor(gb[:, :], gbias[:, :, 0], gbias[:, :, 1], ALU.add).then_inc(gbias_sum, 1)

            def scale(k, src, f):
                V.tensor_scalar(gws[:, k, :], gw[:, src, :], f, None, ALU.mult).then_inc(weights_scaled, 1)

            scale(0, 3, 0.25)
            scale(1, 3, -0.5)
            V.tensor_scalar(Q4[:, :], h0, 4.0, None, ALU.mult).then_inc(q_rdy, 1)
            V.memset(P2[:, :], 0.0).then_inc(p_rdy, 1)
            V.memset(G[:, :, :], 0.0).then_inc(acc_done, 1)
            dve.wait_ge(acc_done, 1)
            V.tensor_scalar(G[:, :, STEPS - 1], h0, 2.0, None, ALU.mult).then_inc(g_rdy, 1)
            scale(2, 4, 0.5)
            scale(3, 5, 0.25)
            scale(4, 6, 0.5)
            V.memset(bank[4][:, :], 0.0).then_inc(up_ps, 1)
            def yt_evac(s):
                dve.wait_ge(yt_ps, s)
                V.tensor_scalar(yT[:, :], ps_misc[:, 0:P], qbias, None, ALU.add).then_inc(yt_done, 1)

            oh_loop, oh_last = [o[:, :] for o in oh_cur], [o[:, SLOTS - 1, :] for o in oh]
            A_loop, A_last = [o[:, :] for o in A_cur], [o[:, SLOTS - 1, :] for o in A]

            def route_step(s, k, oh_to=oh_loop):
                if k == 0:
                    dve.wait_ge(lg_ps, s)
                    V.tensor_copy(lg[:, :], ps_misc[:, 0:E0])
                    o = V.max(out=top8[:, :], in_=ps_misc[:, 0:E0])
                else:
                    dve.wait_ge(route, N_ROUTE * (s - 1) + k)
                if k == 1:
                    V.tensor_tensor(gap[:, :], top8[:, 0:1], top8[:, 1:2], ALU.subtract)
                    o = V.max_index(out=idx8[:, :], in_max=top8[:, :], in_values=lg[:, :])
                if k == 2:
                    o = V.tensor_copy(idxf[:, :], idx8[:, 0:2])
                if k in (3, 4):
                    o = V.tensor_scalar(oh_to[k - 3], iota8, idxf[:, k - 3:k - 2], None, ALU.is_equal)
                if k == 5:
                    o = V.tensor_tensor(cnt[:, bass.ds(s, 1), :], oh_to[0].unsqueeze(1), oh_to[1].unsqueeze(1), ALU.add)
                if k >= 6:
                    o = V.tensor_copy(oh[k - 6][:, bass.ds(s, 1), :], oh_to[k - 6].unsqueeze(1))
                o.then_inc(route, 1)

            def count_before(s):
                V.tensor_tensor(pref[:, bass.ds(s + 1, 1), :], pref[:, bass.ds(s, 1), :], cnt[:, bass.ds(s, 1), :],
                                ALU.add).then_inc(pref_done, 1)

            def gates(s, k):
                dve.wait_ge(gap_act, s)
                V.tensor_scalar(gate[k][:, bass.ds(s, 1)], tgap[:, :], 0.5 - k, 0.5, ALU.mult, ALU.add)

            def keep_sum(s, k):
                V.tensor_copy(A[k][:, bass.ds(s, 1), :], A_cur[k][:, :].unsqueeze(1))

            def accumulate(s, e, k, in_loop=False, y=ps_y, A_to=A_loop, chosen_by=oh_loop):
                o = A_to[k]
                w = chosen_by[k][:, e:e + 1]
                if k == 0:
                    dve.wait_ge(down_ps, down_cnt(s, e))
                    if not in_loop:
                        dve.wait_ge(acc_done, down_cnt(s, e - 1))
                if e == 0:
                    r = V.tensor_scalar(o, y, w, None, ALU.mult)
                else:
                    r = V.scalar_tensor_tensor(out=o, in0=y, scalar=w, in1=o, op0=ALU.mult, op1=ALU.add)
                if k == 1:
                    r.then_inc(acc_done, 1)

            def side(i, t, half):
                if (t, half) == (0, 1):
                    yt_evac(i)
                if t % 4 == 2:
                    e = t // 4 - 2
                    accumulate(i if e >= 0 else i - 1, e % E0, half, in_loop=True)
                for k, at in enumerate(((3, 0), (3, 1), (4, 1), (7, 1), (8, 1), (9, 1), (11, 1), (12, 1))):
                    if at == (t, half):
                        route_step(i, k)
                if half == 1 and t in (7, 8):
                    keep_sum(i - 1, t - 7)
                if half == 1 and t in (13, 16):
                    gates(i, int(t == 16))
                if (t, half) == (15, 1):
                    count_before(i)

            def gru_block(i, side):
                for t in range(STEPS):
                    n = i * STEPS + t
                    Gp = G[:, :, (t - 1) % STEPS]
                    dve.wait_ge(r_act, n + 1)
                    dve.wait_ge(g_rdy, n + 1)
                    V.scalar_tensor_tensor(out=RH4[:, :], in0=tr[:, :], scalar=1.0, in1=Gp, op0=ALU.add, op1=ALU.mult).then_inc(rh_rdy, 1)
                    dve.wait_ge(z_act, n + 1)
                    V.scalar_tensor_tensor(out=Q4[:, :], in0=tz[:, :], scalar=1.0, in1=Gp, op0=ALU.add, op1=ALU.mult).then_inc(q_rdy, 1)
                    side(i, t, 0)
                    dve.wait_ge(h_act, n + 1)
                    V.scalar_tensor_tensor(out=P2[:, :], in0=tz[:, :], scalar=-1.0, in1=ht[:, :], op0=ALU.add, op1=ALU.mult).then_inc(p_rdy, 1)
                    dve.wait_ge(p_rdy, n + 2)
                    if t == 0 and side is not no_side:
                        dve.wait_ge(yt_ps, i)
                    V.scalar_tensor_tensor(out=G[:, :, t], in0=Q4[:, :], scalar=0.5, in1=P2[:, :], op0=ALU.mult, op1=ALU.subtract).then_inc(g_rdy, 1)
                    side(i, t, 1)

            def no_side(i, t, half):
                pass

            gru_block(0, no_side)
            dve.wait_ge(in_moe, 16 * N_MOE_IN)
            dve.wait_ge(in_x, 16)
            dve.wait_ge(pool_set, 1)
            with dve.Fori(1, BLOCKS) as i:
                gru_block(i, side)

            last = SLOTS - 1
            yt_evac(last)
            for k in range(2):
                accumulate(last - 1, 6, k)
            for k in range(6):
                route_step(last, k, oh_last)
            dve.wait_ge(route, N_ROUTE * (last - 1) + 6)
            dve.wait_ge(pref_done, BLOCKS - 1)
            count_before(last)
            for k in range(2):
                accumulate(last - 1, 7, k, y=ps_y2[1])
            dve.wait_ge(acc_done, down_cnt(last - 1, 7))
            for k in range(2):
                keep_sum(last - 1, k)
            for k in range(2):
                gates(last, k)
            dve.wait_ge(pos_ps, 1)
            V.tensor_scalar(kept[:, :, :], ps_misc[:, 0:BLOCKS * E0].rearrange("p (k e) -> p k e", e=E0), float(CAP), None,
                            ALU.is_lt).then_inc(keep_done, 1)
            dve.wait_ge(keep_done, 1)
            for k in range(2):
                V.tensor_tensor(kd[k][:, :, :], kept[:, :, :], oh[k][:, 1:, :], ALU.mult).then_inc(keep_done, 1)
            for k in range(2):
                dve.wait_ge(keep_done, 2 + k)
                V.tensor_reduce(kg[k][:, :], kd[k][:, :, :], AX_X, ALU.add).then_inc(keep_done, 1)
            for k in range(2):
                dve.wait_ge(keep_done, 4 + k)
                V.tensor_tensor(kg[k][:, :], kg[k][:, :], gate[k][:, 1:], ALU.mult).then_inc(keep_done, 1)
            for k in range(2):
                V.tensor_tensor(kd[k][:, :, :], kd[k][:, :, :], gate[k][:, 1:].unsqueeze(2).to_broadcast([P, BLOCKS, E0]),
                                ALU.mult).then_inc(keep_done, 1)
            dve.wait_ge(keep_done, 9)
            V.tensor_tensor(ck[:, :, :], kd[0][:, :, :], kd[1][:, :, :], ALU.add).then_inc(keep_last, 1)

            def x1_evac(k):
                steps = slice(KCONV - 1 + k * STEPS, KCONV - 1 + (k + 1) * STEPS)
                dve.wait_ge(x1_ps, k + 1)
                V.tensor_tensor(x1p[:, :, steps], bank[k % 2][:, 0:P].rearrange("p (b t) -> p b t", b=B),
                                x_sb[:, k * P:(k + 1) * P].rearrange("p (b t) -> p b t", b=B), ALU.add).then_inc(x1_done, 1)

            def convolve(piece):
                lo, hi = CONV[piece]
                for k in range(KCONV):
                    src, dst = x1p[:, :, k + lo:k + hi], conv[:, :, lo:hi]
                    if k == 0:
                        dve.wait_ge(x1_done, hi // STEPS)
                        o = V.tensor_scalar(dst, src, h0[:, 0:1], cb[:, 0:1], ALU.mult, ALU.add)
                    else:
                        dve.wait_ge(conv_step, piece * KCONV + k)
                        o = V.scalar_tensor_tensor(out=dst, in0=src, scalar=h0[:, k:k + 1], in1=dst, op0=ALU.mult, op1=ALU.add)
                    o.then_inc(conv_step, 1)

            dve.wait_ge(keep_done, 7)
            dve.wait_ge(in_rec, 16 * N_REC_IN)
            for e in range(E0):
                for k in range(2):
                    accumulate(last, e, k, y=ps_y2[e % 2], A_to=A_last, chosen_by=oh_last)
                if e == 0:
                    dve.wait_ge(ckt_ps, 1)
                    V.tensor_copy(ckT[:, :], bank[7][0:BLOCKS * E0, 0:P]).then_inc(ckt_done, 1)
                    for j in range(2):
                        V.tensor_scalar(diag[j][:, :], ident, kg[j][:, BLOCKS - 1:], None, ALU.mult).then_inc(diag_done, 1)
                if e >= 1:
                    x1_evac(e - 1)
                if e in (2, 4, 6):
                    convolve(e // 2 - 1)
            convolve(3)
            x1_evac(BLOCKS - 1)
            convolve(4)
            dve.wait_ge(dec_act, 4)
            V.tensor_tensor(sp_v[:, :], sp_t[:, :], sp_r[:, :], ALU.add).then_inc(dec_dve, 1)
            dve.wait_ge(dec_dve, 1)
            V.tensor_tensor(decay[:, :], sp_v[:, 0:1], sp_v[:, 1:2], ALU.mult).then_inc(dec_dve, 1)
            dve.wait_ge(dec_dve, 2)
            V.tensor_scalar(decay[:, :], decay[:, :], -1.0, 1.0, ALU.mult, ALU.add).then_inc(dec_dve, 1)
            dve.wait_ge(dec_dve, 3)
            V.tensor_copy(decay_row[:, :], decay[:, 0:1].to_broadcast([P, T])).then_inc(dec_dve, 1)
            dve.wait_ge(sp_act, 1)
            V.tensor_scalar(Bg[:, :], bank[6][:, :], bpb[:, 0:1], 0.0, ALU.add, ALU.max).then_inc(relu_done, 1)
            dve.wait_ge(relu_done, 1)
            dve.wait_ge(sp_act, 3)
            V.tensor_tensor(Bg[:, :], Bg[:, :], Bt[:, :], ALU.add).then_inc(rec, 1)
            dve.wait_ge(rec, 1)
            dve.wait_ge(u_ps, 1)
            V.scalar_tensor_tensor(out=U[:, :], in0=bank[7][:, :], scalar=bs[:, 0:1], in1=Bg[:, :],
                                   op0=ALU.add, op1=ALU.mult).then_inc(rec, 1)
            dve.wait_ge(rec, 2)
            for b in range(2):
                V.tensor_tensor_scan(S[:, b * T:(b + 1) * T], decay_row[:, :], U[:, b * T:(b + 1) * T], 0.0,
                                     ALU.mult, ALU.add).then_inc(rec, 1)
            dve.wait_ge(c_act, 1)
            for b in range(2):
                dve.wait_ge(rec, 3 + b)
                cols = slice(b * T, (b + 1) * T)
                V.scalar_tensor_tensor(out=Yg[:, cols], in0=S[:, cols], scalar=sp_v[:, 1:2], in1=Cg[:, cols],
                                       op0=ALU.mult, op1=ALU.mult).then_inc(rec, 1)

            def chained(o):
                rt_n[0] += 1
                o.then_inc(rt, 1)
                dve.wait_ge(rt, rt_n[0])

            rt_n = [0]
            dve.wait_ge(in_l1, 16 * N_L1_IN)
            V.tensor_copy(earlier_bf[:, :], earlier)
            dve.wait_ge(rl_ps, 1)
            chained(V.tensor_tensor(pr_e[:, :, :], bank[4][:, 0:TILES * 7].rearrange("p (m e) -> p m e", e=7),
                                    rb[:, :].unsqueeze(1).to_broadcast([P, TILES, 7]), ALU.add))
            chained(V.tensor_scalar(pr_e[:, :, :], pr_e[:, :, :], 50.0, -50.0, ALU.min, ALU.max))
            dve.wait_ge(e_act, 1)
            chained(V.tensor_scalar(pr_e[:, :, :], pr_e[:, :, :], 1.0, None, ALU.add))
            chained(V.reciprocal(prob[:, :, 0:7], pr_e[:, :, :]))
            for m in range(TILES):
                o = V.max(out=ptop[:, m, :], in_=prob[:, m, :])
            chained(o)
            for m in range(TILES):
                o = V.max_index(out=pidx[:, m, :], in_max=ptop[:, m, :], in_values=prob[:, m, :])
            chained(o)
            chained(V.tensor_copy(pidf[:, :], pidx[:, :, 0]))
            V.tensor_tensor(chosen[:, :, :], pidf[:, :].unsqueeze(2).to_broadcast([P, TILES, 8]),
                            iota8.unsqueeze(1).to_broadcast([P, TILES, 8]), ALU.is_equal).then_inc(chosen_done, 1)

            def gated(k):
                g = k // IC1
                dve.wait_ge(g3_ps, k + 1)
                dve.wait_ge(silu_done, k + 1)
                V.tensor_tensor(hh[:, g, k % IC1, :], sg[:, k % 2, :], bank[k % 2 * 2 + 1][:, :], ALU.mult).then_inc(hh_done, 1)

            def add_shared(g):
                dve.wait_ge(out_ps, g + 1)
                for m in range(MPG):
                    M = g * MPG + m
                    V.scalar_tensor_tensor(out=acc[:, M, :], in0=bank[6 + g][:, m * P:(m + 1) * P],
                                           scalar=pshared[:, M:M + 1], in1=acc[:, M, :], op0=ALU.mult,
                                           op1=ALU.add).then_inc(acc2, 1)

            chained(V.tensor_scalar(pw[:, :], ptop[:, :, 0], 1e-8, 1.0 - 1e-8, ALU.max, ALU.min))
            chained(V.tensor_scalar(ptw[:, :], pw[:, :], 0.5, 1e-8, ALU.add, ALU.add))
            chained(V.tensor_scalar(ptw[:, :], ptw[:, :], 0.5, 2.0, ALU.max, ALU.min))
            chained(V.reciprocal(prt[:, :], ptw[:, :]))
            V.tensor_tensor(psel, pw[:, :], prt[:, :], ALU.mult).then_inc(psel_done, 1)
            chained(V.tensor_scalar(pshared[:, :], prt[:, :], 0.5, None, ALU.mult))

            gated(0)
            gated(1)
            counts = bank[5][:, 0:(TILES + 1) * 8].rearrange("p (m e) -> p m e", e=8)
            dve.wait_ge(place_ps, 1)
            chained(V.tensor_tensor(over[:, :, :], counts[:, TILES, :].unsqueeze(2).to_broadcast([P, 8, 8]),
                                    firsts[:, 0:8].unsqueeze(1).to_broadcast([P, 8, 8]), ALU.is_gt))
            chained(V.tensor_reduce(blocks_of[:, :], over[:, :, :], AX_X, ALU.add))
            chained(V.tensor_tensor_scan(blocks_to[:, :], ones8[:, :], blocks_of[:, :], 0.0, ALU.mult, ALU.add))
            chained(V.tensor_tensor(base[:, :], blocks_to[:, :], blocks_of[:, :], ALU.subtract))
            chained(V.scalar_tensor_tensor(out=place[:, :, :], in0=base[:, :].unsqueeze(1).to_broadcast([P, TILES, 8]),
                                           scalar=float(P), in1=counts[:, 0:TILES, :], op0=ALU.mult, op1=ALU.add))
            chained(V.tensor_tensor(place[:, :, :], place[:, :, :], chosen[:, :, :], ALU.mult))
            chained(V.tensor_reduce(row_f[:, :], place[:, :, :], AX_X, ALU.add))
            gated(2)
            chained(V.tensor_tensor(above[:, :, :], row_f[:, :].unsqueeze(2).to_broadcast([P, TILES, 16]),
                                    firsts.unsqueeze(1).to_broadcast([P, TILES, 16]), ALU.is_ge))
            chained(V.tensor_reduce(blk_f[:, :], above[:, :, 1:], AX_X, ALU.add))
            chained(V.scalar_tensor_tensor(out=lane[:, :], in0=blk_f[:, :], scalar=-float(P), in1=row_f[:, :],
                                           op0=ALU.mult, op1=ALU.add))
            chained(V.tensor_tensor(blk1[:, :, :], above[:, :, 0:SORTED], above[:, :, 1:SORTED + 1], ALU.subtract))
            gated(3)
            V.tensor_scalar(token2[:, :, 0, :], blk1[:, :, :], part, None, ALU.mult)
            V.scalar_tensor_tensor(out=token2[:, :, 1, :], in0=iota8.unsqueeze(2).to_broadcast([P, TILES, SORTED]),
                                   scalar=1.0, in1=blk1[:, :, :], op0=ALU.add, op1=ALU.mult)
            V.tensor_tensor(lane1[:, :, :], lane[:, :].unsqueeze(2).to_broadcast([P, TILES, P]),
                            iota128.unsqueeze(1).to_broadcast([P, TILES, P]), ALU.is_equal).then_inc(sort_in, 1)
            dve.wait_ge(token_ps, 1)
            chained(V.tensor_copy(missing[:, :], bank[5][:, P + SORTED:P + 2 * SORTED]))
            chained(V.scalar_tensor_tensor(out=token_t[:, :], in0=missing[:, :], scalar=float(P),
                                           in1=bank[5][:, P:P + SORTED], op0=ALU.mult, op1=ALU.add))
            V.tensor_scalar(source[:, :], token_t[:, :], -float(P), 0.0, ALU.add, ALU.max).then_inc(rows_known, 1)
            chained(V.scalar_tensor_tensor(out=missing[:, :], in0=token_t[:, :], scalar=float(P), in1=trash,
                                           op0=ALU.is_lt, op1=ALU.mult))
            V.scalar_tensor_tensor(out=target[:, :], in0=token_t[:, :], scalar=-float(P), in1=missing[:, :],
                                   op0=ALU.add, op1=ALU.add).then_inc(rows_known, 1)
            gated(4)
            chained(V.tensor_tensor(passed[:, :, :], iota16[0:1, 0:SORTED].unsqueeze(2).to_broadcast([1, SORTED, 8]),
                                    blocks_to[0:1, :].unsqueeze(1).to_broadcast([1, SORTED, 8]), ALU.is_ge))
            chained(V.tensor_reduce(block_expert_f[:, :], passed[:, :, :], AX_X, ALU.add))
            V.tensor_scalar(block_expert[:, :], block_expert_f[:, :], float(E1 - 2), None, ALU.min).then_inc(expert_known, 1)
            gated(5)
            def own_v1(j):
                if j == 0:
                    dve.wait_ge(expert_known, 1)
                if j >= 2:
                    dve.wait_ge(s1_ps, j - 1)
                expert = dve.value_load(block_expert[0:1, j:j + 1], min_val=0, max_val=E1 - 2)
                V.tensor_copy(vb[:, j % 2, 0, 0:I1].unsqueeze(1), v1[:, bass.ds(expert, 1), 0:I1]).then_inc(vb1_done, 1)

            own_v1(0)
            dve.wait_ge(res_done, 2)
            add_shared(0)
            own_v1(1)
            add_shared(1)

            def sorted_evac(j):
                dve.wait_ge(s_out, j + 1)
                if j == 0:
                    dve.wait_ge(stored, 48)
                V.tensor_scalar(ys[:, j, :], bank[6 + j % 2][:, 0:P], xs[:, j, D:], None, ALU.mult).then_inc(ys_done, 1)

            for j in range(SORTED):
                if j < 2:
                    dve.wait_ge(out_ps, j + 1)
                else:
                    dve.wait_ge(s_out, j - 1)
                dve.wait_ge(s3_ps, j + 1)
                dve.wait_ge(s_silu, j + 1)
                V.tensor_tensor(hh[:, j % 2, :, 0:P], sg[:, j % 2, 0:IC1 * P].rearrange("p (c t) -> p c t", t=P),
                                bank[j % 2 * 2 + 1][:, 0:IC1 * P].rearrange("p (c t) -> p c t", t=P), ALU.mult).then_inc(s_hh, 1)
                if j + 2 < SORTED:
                    own_v1(j + 2)
                if j >= 1:
                    sorted_evac(j - 1)
            sorted_evac(SORTED - 1)


def kernel(**inputs):
    import numpy as np
    import concourse.bacc as bacc
    from concourse.bass_utils import run_bass_kernel_spmd

    f = {k: np.asarray(v) for k, v in inputs.items()}
    c = lambda v: np.ascontiguousarray(v)
    L0, L1, M0, M1 = "L0_cond_", "L1_cond_", "L0_ffn_", "L1_ffn_"
    col = lambda v: v.reshape(-1, 1)
    tok = np.arange(P)
    b_of, t_of = tok // STEPS, tok % STEPS
    sortc = np.concatenate([tok[:, None] < tok[None, :], np.broadcast_to(tok, (P, P)),
                            np.broadcast_to(P * np.arange(16), (P, 16)),
                            P + B * T + tok[:, None] + P * np.arange(SORTED)[None, :],
                            np.zeros((P, P - 16 - SORTED)), tok[:, None]], 1).astype(np.float32)
    same = b_of[:, None] == b_of[None, :]
    before = same & (t_of[:, None] < t_of[None, :])
    below = b_of[:, None] < b_of[None, :]
    v1 = np.concatenate([f[M1 + "ew1"], f[M1 + "sw1"][None]])
    v3 = np.concatenate([f[M1 + "ew3"], f[M1 + "sw3"][None]])
    v2 = np.concatenate([f[M1 + "ew2"], f[M1 + "sw2"][None]])
    fill = IC1 * P - I1
    v1, v3 = (np.pad(v, ((0, 0), (0, fill), (0, 0))) for v in (v1, v3))
    v2 = np.pad(v2, ((0, 0), (0, 0), (0, fill)))
    b2 = np.zeros((BLOCKS, E0, BLOCKS, D), np.float32)
    for k in range(BLOCKS):
        b2[k, :, k] = f[M0 + "b2"]
    b2 = b2.reshape(BLOCKS * E0, BLOCKS, D)
    both = lambda v: c(np.concatenate([v, v]))
    arrays = {
        "gw": c(np.stack([f[L0 + n].T for n in ("Wxr", "Wxz", "Wxh", "Whr", "Whz", "Whh", "Whq")], 1)),
        "small": np.concatenate([*(col(f[L0 + "b" + s + g]) for g in "rzh" for s in "xh"), col(f[L0 + "bhq"]),
                                 f["cond_1024"].T, np.eye(P, dtype=np.float32),
                                 f["x"].reshape(B, BLOCKS, STEPS, D).transpose(3, 1, 0, 2).reshape(D, BLOCKS * P)], 1),
        "consts": c(np.stack([before, same, below], 1).astype(np.float32)),
        "iota16": np.broadcast_to(np.arange(16, dtype=np.float32), (P, 16)).copy(),
        "sortc": sortc,
        "wg": f[M0 + "Wg"],
        "w1": c(f[M0 + "W1"].transpose(1, 0, 2)),
        "b1": c(f[M0 + "b1"].reshape(E0, HC, P).transpose(2, 0, 1)),
        "w2": c(f[M0 + "W2"].reshape(E0, HC, P, D).transpose(2, 0, 1, 3)),
        "b2": b2,
        "wp": f[L1 + "Wp"], "ws": f[L1 + "Ws"], "wo": both(f[L1 + "Wo"]),
        "cb": col(f[L1 + "conv_b"]), "bpb": both(f[L1 + "bp"].reshape(2, NS).T), "bs": both(col(f[L1 + "bs"])), "bo": col(f[L1 + "bo"]),
        "alog": both(np.stack([f[L1 + "A_log"], f[L1 + "dt_log"]], 1)),
        "rw": c(f[M1 + "router_w"].T), "rb": np.broadcast_to(f[M1 + "routing_bias"], (P, 7)).copy(),
        "v1": c(v1.transpose(2, 0, 1)), "v3": c(v3.transpose(2, 0, 1)),
        "v2": c(v2.reshape(E1, D, IC1, P).transpose(3, 0, 2, 1)),
    }
    nc = bacc.Bacc("TRN2", target_bir_lowering=False, num_devices=1)
    args = {k: nc.dram_tensor("in_" + k, v.shape, F32, kind="ExternalInput").ap() for k, v in arrays.items()}
    out = nc.dram_tensor("out", (B * T + SORTED * P, D), F32, kind="ExternalOutput").ap()
    adaln_ffn_kernel(nc, args, out)
    r = run_bass_kernel_spmd(nc, [{"in_" + k: v for k, v in arrays.items()}], core_ids=[0])
    return np.asarray(r.results[0]["out"])[:B * T].reshape(B, T, D)
```
